# Optimizing a Trainium2 kernel written in Bass

```python
import numpy as np
import jax
import jax.numpy as jnp

def _softmax(x, axis=-1):
    return jax.nn.softmax(x, axis=axis)

def _gelu(x):
    return jax.nn.gelu(x, approximate=True)

def _silu(x):
    return jax.nn.silu(x)

def _sigmoid(x):
    return jax.nn.sigmoid(x)

def _layernorm(x, axis=-1, eps=1e-05):
    m = jnp.mean(x, axis=axis, keepdims=True)
    v = jnp.var(x, axis=axis, keepdims=True)
    return (x - m) / jnp.sqrt(v + eps)

def _scatter_add(tgt, idx, src, axis=0):
    return tgt.at[idx].add(src)

def _segment_sum(src, seg, n):
    return jax.ops.segment_sum(src, seg, n)
kernel_name = 'mk_gnn_preln_d4_gnn_r8_beb307'

def setup_inputs(seed: int=0):
    np.random.seed(seed)
    _w = jnp.asarray

    def _rec_inputs():
        import jax
        import jax.numpy as jnp
        _gk = jax.random.key(seed)
        x = -0.0001006 + 1 * jax.random.normal(jax.random.fold_in(_gk, 1), (12500, 48), jnp.float32)
        src = jax.random.randint(jax.random.fold_in(_gk, 2), (200000,), 0, 12500, jnp.int32)
        dst = jax.random.randint(jax.random.fold_in(_gk, 3), (200000,), 0, 12500, jnp.int32)
        _o = jnp.argsort(dst, stable=True)
        src = src[_o]
        dst = dst[_o]
        edge_attr_16 = 0.000196303 + 1.00016 * jax.random.normal(jax.random.fold_in(_gk, 12), (200000, 16), jnp.float32)
        edge_attr_32 = 0.000189758 + 1.00013 * jax.random.normal(jax.random.fold_in(_gk, 13), (200000, 32), jnp.float32)
        edge_weight1 = -0.000414295 + 0.999828 * jax.random.normal(jax.random.fold_in(_gk, 15), (200000, 1), jnp.float32)
        return (x, src, dst, edge_attr_16, edge_attr_32, edge_weight1)
    x, src, dst, edge_attr_16, edge_attr_32, edge_weight1 = _rec_inputs()

    def _L0_gnn_setup():
        import jax, jax.numpy as jnp
        import numpy as np
        N_NODES = 12500
        key = jax.random.key(seed)
        k1, k2, k3, k4, k5, k6 = jax.random.split(key, 6)
        node_dim, edge_dim, hidden = (48, 32, 128)
        E = 200000
        x = jax.random.normal(k1, (N_NODES, node_dim), dtype=jnp.float32)
        edge_index = jax.random.randint(k2, (2, E), 0, N_NODES, dtype=jnp.int64)
        edge_attr = jax.random.normal(k3, (E, edge_dim), dtype=jnp.float32)
        in_dim = 2 * node_dim + edge_dim
        s1 = 1.0 / np.sqrt(in_dim)
        s2 = 1.0 / np.sqrt(hidden)
        W1 = jax.random.uniform(k4, (in_dim, hidden), minval=-s1, maxval=s1, dtype=jnp.float32)
        b1 = jax.random.uniform(k5, (hidden,), minval=-s1, maxval=s1, dtype=jnp.float32)
        W2 = jax.random.uniform(k6, (hidden, node_dim), minval=-s2, maxval=s2, dtype=jnp.float32)
        b2 = jnp.zeros((node_dim,), dtype=jnp.float32)
        return {'x': x, 'edge_index': edge_index, 'edge_attr': edge_attr, 'W1': W1, 'b1': b1, 'W2': W2, 'b2': b2}
    _L0_gnn_all = _L0_gnn_setup()
    _L0_gnn_in = {k: v for k, v in _L0_gnn_all.items() if k in ('W1', 'b1', 'W2', 'b2')}
    del _L0_gnn_all

    def _L1_gnn_setup():
        import jax, jax.numpy as jnp
        import numpy as np
        N_NODES = 12500
        N_EDGES = 200000
        N_CLASSES = 48
        key = jax.random.key(seed)
        k1, k2, k3, k4 = jax.random.split(key, 4)
        soft_label = jax.random.normal(k1, (N_NODES, N_CLASSES), dtype=jnp.float32)
        e = jax.random.normal(k2, (N_EDGES, 1), dtype=jnp.float32)
        src = jax.random.randint(k3, (N_EDGES,), 0, N_NODES)
        dst = jax.random.randint(k4, (N_EDGES,), 0, N_NODES)
        return {'soft_label': soft_label, 'e': e, 'src': src, 'dst': dst}
    _L1_gnn_all = _L1_gnn_setup()
    _L1_gnn_in = {k: v for k, v in _L1_gnn_all.items() if k in ()}
    del _L1_gnn_all

    def _L2_gnn_setup():
        import jax, jax.numpy as jnp
        import numpy as np
        N_NODES = 12500
        N_EDGES = 200000
        IN_FEAT = 48
        OUT_FEAT = 48
        key = jax.random.key(seed)
        k_h, k_src, k_dst, k_tw, k_tb, k_pw, k_pb = jax.random.split(key, 7)
        lim = 1.0 / np.sqrt(IN_FEAT)
        return {'h': jax.random.normal(k_h, (N_NODES, IN_FEAT), dtype=jnp.float32), 'theta_w': jax.random.uniform(k_tw, (OUT_FEAT, IN_FEAT), jnp.float32, -lim, lim), 'theta_b': jax.random.uniform(k_tb, (OUT_FEAT,), jnp.float32, -lim, lim), 'phi_w': jax.random.uniform(k_pw, (OUT_FEAT, IN_FEAT), jnp.float32, -lim, lim), 'phi_b': jax.random.uniform(k_pb, (OUT_FEAT,), jnp.float32, -lim, lim), 'src': jax.random.randint(k_src, (N_EDGES,), 0, N_NODES, dtype=jnp.int64), 'dst': jax.random.randint(k_dst, (N_EDGES,), 0, N_NODES, dtype=jnp.int64)}
    _L2_gnn_all = _L2_gnn_setup()
    _L2_gnn_in = {k: v for k, v in _L2_gnn_all.items() if k in ('theta_w', 'theta_b', 'phi_w', 'phi_b')}
    del _L2_gnn_all

    def _L3_gnn_setup():
        import jax, jax.numpy as jnp
        import numpy as np
        N_NODES = 12500
        N_EDGES = 200000
        N_FEAT = 48
        N_EDGE_FEAT = 16
        HIDDEN = 128
        key = jax.random.key(seed)
        ks = jax.random.split(key, 8)
        tot = 2 * N_FEAT + N_EDGE_FEAT
        s1 = 1.0 / np.sqrt(tot)
        s2 = 1.0 / np.sqrt(HIDDEN)
        return {'x': jax.random.normal(ks[0], (N_NODES, N_FEAT), dtype=jnp.float32), 'edge_index': jax.random.randint(ks[1], (2, N_EDGES), 0, N_NODES, dtype=jnp.int64), 'edge_feat': jax.random.normal(ks[2], (N_EDGES, N_EDGE_FEAT), dtype=jnp.float32), 'W1': jax.random.normal(ks[3], (tot, HIDDEN), dtype=jnp.float32) * s1, 'b1': jnp.zeros((HIDDEN,), dtype=jnp.float32), 'W2': jax.random.normal(ks[4], (HIDDEN, HIDDEN), dtype=jnp.float32) * s2, 'b2': jnp.zeros((HIDDEN,), dtype=jnp.float32), 'W3': jax.random.normal(ks[5], (HIDDEN, N_FEAT), dtype=jnp.float32) * s2, 'b3': jnp.zeros((N_FEAT,), dtype=jnp.float32)}
    _L3_gnn_all = _L3_gnn_setup()
    _L3_gnn_in = {k: v for k, v in _L3_gnn_all.items() if k in ('W1', 'b1', 'W2', 'b2', 'W3', 'b3')}
    del _L3_gnn_all
    return {'x': x, 'src': src, 'dst': dst, 'edge_attr_16': edge_attr_16, 'edge_attr_32': edge_attr_32, 'edge_weight1': edge_weight1, 'L0_gnn_W1': _L0_gnn_in['W1'], 'L0_gnn_b1': _L0_gnn_in['b1'], 'L0_gnn_W2': _L0_gnn_in['W2'], 'L0_gnn_b2': _L0_gnn_in['b2'], 'L2_gnn_theta_w': _L2_gnn_in['theta_w'], 'L2_gnn_theta_b': _L2_gnn_in['theta_b'], 'L2_gnn_phi_w': _L2_gnn_in['phi_w'], 'L2_gnn_phi_b': _L2_gnn_in['phi_b'], 'L3_gnn_W1': _L3_gnn_in['W1'], 'L3_gnn_b1': _L3_gnn_in['b1'], 'L3_gnn_W2': _L3_gnn_in['W2'], 'L3_gnn_b2': _L3_gnn_in['b2'], 'L3_gnn_W3': _L3_gnn_in['W3'], 'L3_gnn_b3': _L3_gnn_in['b3']}

def reference(x, src, dst, edge_attr_16, edge_attr_32, edge_weight1, L0_gnn_W1, L0_gnn_b1, L0_gnn_W2, L0_gnn_b2, L2_gnn_theta_w, L2_gnn_theta_b, L2_gnn_phi_w, L2_gnn_phi_b, L3_gnn_W1, L3_gnn_b1, L3_gnn_W2, L3_gnn_b2, L3_gnn_W3, L3_gnn_b3):
    import jax
    import jax.numpy as jnp

    def _L0_gnn_ref(x, edge_index, edge_attr, W1, b1, W2, b2):
        import jax, jax.numpy as jnp
        import numpy as np
        N_NODES = 12500
        src, dst = (edge_index[0], edge_index[1])
        x_i = x[dst]
        x_j = x[src]
        tmp = jnp.concatenate([x_i, x_j, edge_attr], axis=1)
        h = jax.nn.relu(tmp @ W1 + b1)
        msg = h @ W2 + b2
        out = jax.ops.segment_sum(msg, dst, num_segments=N_NODES)
        return out

    def _L1_gnn_ref(soft_label, e, src, dst):
        import jax, jax.numpy as jnp
        import numpy as np
        N_NODES = 12500
        N_EDGES = 200000
        N_CLASSES = 48
        N = soft_label.shape[0]
        logits = e[:, 0]
        seg_max = jax.ops.segment_max(logits, dst, num_segments=N)
        seg_max = jnp.where(jnp.isfinite(seg_max), seg_max, 0.0)
        ex = jnp.exp(logits - seg_max[dst])
        seg_sum = jax.ops.segment_sum(ex, dst, num_segments=N)
        a = ex / seg_sum[dst]
        msg = soft_label[src] * a[:, None]
        rst = jax.ops.segment_sum(msg, dst, num_segments=N)
        return jax.nn.elu(rst)

    def _L2_gnn_ref(h, theta_w, theta_b, phi_w, phi_b, src, dst):
        import jax, jax.numpy as jnp
        import numpy as np
        N_NODES = 12500
        N_EDGES = 200000
        IN_FEAT = 48
        OUT_FEAT = 48
        phi_all = h @ phi_w.T + phi_b
        diff = h[dst] - h[src]
        e = diff @ theta_w.T + theta_b + phi_all[src]
        out = jax.ops.segment_max(e, dst, num_segments=N_NODES)
        out = jnp.where(jnp.isneginf(out), 0.0, out)
        return out

    def _L3_gnn_ref(x, edge_index, edge_feat, W1, b1, W2, b2, W3, b3):
        import jax, jax.numpy as jnp
        import numpy as np
        N_NODES = 12500
        N_EDGES = 200000
        N_FEAT = 48
        N_EDGE_FEAT = 16
        HIDDEN = 128
        source = edge_index[0]
        target = edge_index[1]
        edge = jnp.concatenate([x[source], x[target], edge_feat], axis=-1)
        h = jax.nn.relu(edge @ W1 + b1)
        h = jax.nn.relu(h @ W2 + b2)
        message = h @ W3 + b3
        n = x.shape[0]
        msum = jax.ops.segment_sum(message, target, num_segments=n)
        cnt = jax.ops.segment_sum(jnp.ones((target.shape[0],), dtype=x.dtype), target, num_segments=n)
        update = msum / jnp.maximum(cnt, 1.0)[:, None]
        return x + update
    edge_index = jnp.stack([src, dst])
    h = jnp.maximum(_layernorm(x, axis=-1), 0.0)
    x = x + _L0_gnn_ref(h, edge_index, edge_attr_32, L0_gnn_W1, L0_gnn_b1, L0_gnn_W2, L0_gnn_b2)
    h = jnp.maximum(_layernorm(x, axis=-1), 0.0)
    x = x + _L1_gnn_ref(h, edge_weight1, src, dst)
    h = jnp.maximum(_layernorm(x, axis=-1), 0.0)
    x = x + _L2_gnn_ref(h, L2_gnn_theta_w, L2_gnn_theta_b, L2_gnn_phi_w, L2_gnn_phi_b, src, dst)
    h = jnp.maximum(_layernorm(x, axis=-1), 0.0)
    x = x + _L3_gnn_ref(h, edge_index, edge_attr_16, L3_gnn_W1, L3_gnn_b1, L3_gnn_W2, L3_gnn_b2, L3_gnn_W3, L3_gnn_b3)
    return x

_drawn_inputs = setup_inputs


def setup_inputs(seed=0):
    import zlib

    import numpy as np

    out = dict(_drawn_inputs(seed))
    spreads = {'L0_gnn_b2': (0.0, 0.1),
     'L3_gnn_b1': (0.0, 0.8),
     'L3_gnn_b2': (0.0, 0.646),
     'L3_gnn_b3': (0.0, 0.343)}
    factors = {'edge_attr_16': 5.512, 'L2_gnn_theta_b': 2.689}
    for name, (base, spread) in spreads.items():
        noise = np.random.default_rng([zlib.crc32(name.encode()), seed]).standard_normal(out[name].shape)
        drawn = base * np.exp(spread * noise) if base else spread * noise
        out[name] = jnp.asarray(drawn.astype(out[name].dtype))
    for name, factor in factors.items():
        out[name] = (out[name] * factor).astype(out[name].dtype)
    return out
```

```python
import concourse.bass as bass
from concourse import mybir
from contextlib import ExitStack

P = 128
D = 48
TJ = 4
CHUNK = P * TJ
CH = 4
GROUP = CH * CHUNK
RING = 2 * CH
NODE_BLOCKS = 7
SEARCH_COLS = 5
BIG = 3.0e38


class Chunk:

    def __init__(self, turn, k):
        self.slot = k % RING
        self.turn = turn + k // RING
        self.n = turn * RING + k
        self.half = self.slot // CH
        self.at_group_start = self.slot % CH == 0
        self.fixed = isinstance(self.n, int)


def pipeline(eng, stages, turns):
    for k in range(RING):
        for lag, stage in stages:
            if k >= lag:
                stage(Chunk(0, k - lag))
    if turns > 1:
        with eng.Fori(1, turns) as turn:
            for k in range(RING):
                for lag, stage in stages:
                    stage(Chunk(turn, k - lag))
    for k in range(max(lag for lag, _ in stages)):
        for lag, stage in stages:
            if k < lag:
                stage(Chunk(turns, k - lag))


def build(nc, x_in, src_in, dst_in, dst_prev_in, heads_in, ea0_in, ea3_in, w_in,
          L0_W1, L0_b1, L0_W2, L0_b2, thetaT_in, phiT_in, theta_b, phi_b,
          L3_W1, L3_b1, L3_W2, L3_b2, L3_W3, L3_b3, out):
    f32, i32, bf16 = mybir.dt.float32, mybir.dt.int32, mybir.dt.bfloat16
    ALU = mybir.AluOpType
    ACT = mybir.ActivationFunctionType
    AX = mybir.AxisListType.X

    N = x_in.shape[0]
    B = N // P
    E = dst_in.shape[0]
    EC = E // P
    ROWS = heads_in.shape[0]
    COLS = E // ROWS
    GROUPS = E // GROUP
    TURNS = GROUPS // 2
    NCH = E // CHUNK
    NQ = B // NODE_BLOCKS
    SB = -(-(B + 1) // SEARCH_COLS) * SEARCH_COLS
    HID = L0_W1.shape[1]
    ZERO_STEP = next(k for k in (7, 6, 5, 3, 2, 1) if EC // 16 % k == 0)
    assert B % NODE_BLOCKS == 0 and GROUPS % 2 == 0 and NCH % RING == 0

    dram = lambda name, shape, dt: nc.dram_tensor(name, shape, dt, kind="Internal").ap()
    widths = [D, D + 1, D, D]
    table = [dram(f"table{l}", (N, widths[l]), f32) for l in range(4)]
    prefix = [dram(f"prefix{l}", (E, widths[l]), f32) for l in range(4)]
    first_rows = dram("first_rows", (E + N, D), f32)
    dstf = dram("dstf", (ROWS, COLS), f32)
    same_row = dram("same_row", (E,), bf16)
    restart_row = dram("restart_row", (E,), bf16)
    decay_row = dram("decay_row", (E,), f32)
    ex_row = dram("ex_row", (E,), f32)
    carry_dram = dram("carry_dram", (3, P), f32)

    ctx = ExitStack()
    with ctx:
        def sb(name, shape, dt=f32):
            return ctx.enter_context(nc.sbuf_tensor(name, shape, dt))

        def sem(name):
            return ctx.enter_context(nc.semaphore(name))

        x = sb("x", [P, B, D])
        h = sb("h", [P, B, D + 1])
        start = sb("start", [P, SB])
        count = sb("count", [P, B])
        filled = sb("filled", [P, B])
        empty = sb("empty", [P, B])
        inv_count = sb("inv_count", [P, B])
        last_edge = sb("last_edge", [P, B], i32)
        first_edge = sb("first_edge", [P, B], i32)
        node_tmp = sb("node_tmp", [P, B])
        ident = sb("ident", [P, P])
        w1_0 = sb("w1_0", [P, HID])
        w1_3 = sb("w1_3", [P, HID])
        w2_0 = sb("w2_0", [P, D])
        w2_3 = sb("w2_3", [P, HID])
        w3_3 = sb("w3_3", [P, D])
        thetaT = sb("thetaT", [D, D])
        phiT = sb("phiT", [D, D])
        wq = sb("wq", [D, D])
        b1_0 = sb("b1_0", [P, 1])
        b1_3 = sb("b1_3", [P, 1])
        b2_3 = sb("b2_3", [P, 1])
        b2_0 = sb("b2_0", [P, 1, D])
        b3_3 = sb("b3_3", [P, 1, D])
        tb = sb("tb", [P, 1, D])
        pb = sb("pb", [P, 1, D])
        eps = sb("eps", [P, 1])
        zeros = sb("zeros", [P, 16 * D])
        e_dst = sb("e_dst", [P, EC], i32)
        e_prev = sb("e_prev", [P, EC], i32)
        e_w = sb("e_w", [P, EC])
        e_start = sb("e_start", [P, EC])
        e_max = sb("e_max", [P, EC])
        e_tmp = sb("e_tmp", [P, EC])
        e_half = sb("e_half", [P, EC], bf16)
        e_half2 = sb("e_half2", [P, EC], bf16)
        row_stat = sb("row_stat", [P, 2])
        carry_row = sb("carry_row", [1, 2, P])
        carry_scan = sb("carry_scan", [1, P + 1])
        carry = sb("carry", [P, 1])
        heads_i = sb("heads_i", [P, ROWS], i32)
        heads = sb("heads", [P, ROWS])
        below = sb("below", [P, ROWS + COLS])
        node_id_i = sb("node_id_i", [P, SB], i32)
        node_id = sb("node_id", [P, SB])
        heads_below = sb("heads_below", [P, SB])
        row_f = sb("row_f", [P, SB])
        row_i = sb("row_i", [P, SB], i32)
        in_row = sb("in_row", [P, SB])
        found = sb("found", [P, 2, SEARCH_COLS, COLS])
        idx = sb("idx", [P, 2, CH * TJ], i32)
        G = sb("G", [P, RING, TJ, 112])
        K = sb("K", [P, RING, CHUNK])
        H1 = sb("H1", [P, 4, CHUNK])
        H2 = sb("H2", [P, 4, CHUNK])
        S = sb("S", [P, 4, CHUNK])
        O = sb("O", [P, RING, TJ * (D + 1)])
        mask_f = sb("mask_f", [P, 2, GROUP])
        mask_h = mask_f[:, :, :].bitcast(bf16)
        ex = sb("ex", [P, 2, CH, TJ])
        R = sb("R", [P, 2, NODE_BLOCKS, D + 1])
        u = sb("u", [P, 2, NODE_BLOCKS, D])
        u2 = sb("u2", [P, 2, NODE_BLOCKS, D])
        ns = sb("ns", [P, 2, 6, NODE_BLOCKS])

        pT = [ctx.enter_context(nc.psum_tensor(f"pT{i}", [P, CHUNK], f32)) for i in range(2)]
        pH1 = [ctx.enter_context(nc.psum_tensor(f"pH1_{i}", [P, CHUNK], f32)) for i in range(2)]
        pH2 = [ctx.enter_context(nc.psum_tensor(f"pH2_{i}", [P, CHUNK], f32)) for i in range(2)]
        pO = [ctx.enter_context(nc.psum_tensor(f"pO{i}", [P, CHUNK], f32)) for i in range(2)]

        weights_in = sem("weights_in")
        edges_in = sem("edges_in")
        w_edge_in = sem("w_edge_in")
        x_loaded = sem("x_loaded")
        heads_loaded = sem("heads_loaded")
        zeros_set = sem("zeros_set")
        rows_zeroed = sem("rows_zeroed")
        ident_set = sem("ident_set")
        ident_done = sem("ident_done")
        node_id_set = sem("node_id_set")
        G_zeroed = sem("G_zeroed")
        dstf_made = sem("dstf_made")
        dstf_stored = sem("dstf_stored")
        same_made = sem("same_made")
        same_stored = sem("same_stored")
        carry_made = sem("carry_made")
        carry_hop = [sem(f"carry_hop{i}") for i in range(4)]
        ex_arg_made = sem("ex_arg_made")
        ex_made = sem("ex_made")
        decay_made = sem("decay_made")
        ex_stored = sem("ex_stored")
        rows_chosen = sem("rows_chosen")
        found_in = [sem(f"found_in{i}") for i in range(2)]
        found_used = sem("found_used")
        places_made = sem("places_made")
        vector_done = sem("vector_done")
        wq_made = sem("wq_made")
        sp_passed = sem("sp_passed")
        pool_passed = sem("pool_passed")
        pe_passed = sem("pe_passed")
        out_made = sem("out_made")
        out_stored = sem("out_stored")
        last_rows_in = {v: [sem(f"last_rows_in{v}_{i}") for i in range(2)] for v in range(1, 5)}
        last_rows_used = {v: sem(f"last_rows_used{v}") for v in range(1, 5)}
        elu_arg = sem("elu_arg")
        elu_exp = sem("elu_exp")
        var_made = [sem(f"var_made{v}") for v in range(4)]
        sd_made = [sem(f"sd_made{v}") for v in range(4)]
        h_made = [sem(f"h_made{v}") for v in range(4)]
        h_stored = [sem(f"h_stored{v}") for v in range(4)]
        h_scattered = {v: sem(f"h_scattered{v}") for v in (0, 3)}
        hT_made = sem("hT_made")
        hT_copied = sem("hT_copied")
        theta_h = sem("theta_h")
        def per_layer(name, layers=(0, 1, 2, 3)):
            return {l: sem(f"{name}{l}") for l in layers}

        def per_half(name, layers):
            return {l: [sem(f"{name}{l}_{i}") for i in range(2)] for l in layers}

        MLP = (0, 3)
        idx_in = [sem(f"idx_in{i}") for i in range(2)]
        first_in = per_half("first_in", MLP)
        mask_in = [sem(f"mask_in{i}") for i in range(2)]
        ea_in = per_half("ea_in", MLP)
        ex_in = per_half("ex_in", (1,))
        gathered = [sem(f"gathered{i}") for i in range(RING)]
        weighted = per_layer("weighted", (1,))
        transposed = per_layer("transposed")
        src_copied = per_layer("src_copied", (0, 2, 3))
        dst_spread = per_layer("dst_spread", MLP)
        hidden1 = per_layer("hidden1_", (0, 2, 3))
        relu1 = per_layer("relu1_", MLP)
        hidden2 = per_layer("hidden2_", (3,))
        relu2 = per_layer("relu2_", (3,))
        scanned = per_layer("scanned")
        rows_made = per_layer("rows_made")
        rows_copied = per_layer("rows_copied")
        rows_stored = [sem(f"rows_stored{i}") for i in range(2)]

        KROWS = {0: 128, 3: 112}
        def column(v):
            return v.rearrange("(h o) -> h o", o=1)

        def on_all(v):
            return v.rearrange("(o d) -> o d", o=1).to_broadcast([P, D])

        weight_loads = [
            (w1_0[0:48, :], L0_W1[48:96, :]), (w1_0[48:64, :], L0_W1[96:112, :]),
            (w1_0[64:112, :], L0_W1[0:48, :]), (w1_0[112:128, :], L0_W1[112:128, :]),
            (w1_3[0:48, :], L3_W1[0:48, :]), (w1_3[48:64, :], L3_W1[96:112, :]),
            (w1_3[64:112, :], L3_W1[48:96, :]),
            (w2_0[:, :], L0_W2), (w2_3[:, :], L3_W2), (w3_3[:, :], L3_W3),
            (thetaT[:, :], thetaT_in), (phiT[:, :], phiT_in),
            (b1_0[:, :], column(L0_b1)), (b1_3[:, :], column(L3_b1)), (b2_3[:, :], column(L3_b2)),
            (b2_0[:, 0, :], on_all(L0_b2)), (b3_3[:, 0, :], on_all(L3_b3)),
            (tb[:, 0, :], on_all(theta_b)), (pb[:, 0, :], on_all(phi_b)),
        ]
        ALL_WEIGHTS = 16 * len(weight_loads)

        block = ctx.enter_context(nc.Block())

        @block.sync
        def _(sp):
            sp.dma_start(e_dst[:, :], dst_in.rearrange("(p c) -> p c", p=P)).then_inc(edges_in, 16)
            sp.dma_start(e_prev[:, :], dst_prev_in.rearrange("(p c) -> p c", p=P)).then_inc(edges_in, 16)
            sp.dma_start(heads_i[:, :], heads_in.rearrange("(o r) -> o r", o=1).to_broadcast([P, ROWS]))\
              .then_inc(heads_loaded, 16)
            sp.dma_start(x[:, :, :], x_in.rearrange("(p b) d -> p b d", p=P)).then_inc(x_loaded, 16)
            sp.dma_start(e_w[:, :], w_in.rearrange("(p c) -> p c", p=P)).then_inc(w_edge_in, 16)
            sp.wait_ge(dstf_made, 1)
            sp.dma_start(dstf.rearrange("r c -> (r c)").rearrange("(p c) -> p c", p=P), e_tmp[:, :])\
              .then_inc(dstf_stored, 16)
            sp.wait_ge(zeros_set, 1)
            sp.wait_ge(dstf_stored, 16)
            zero_view = first_rows[0:E, :].rearrange("(p r q) d -> p r (q d)", p=P, q=16)
            for r in range(0, EC // 16, ZERO_STEP):
                sp.dma_start(zero_view[:, r:r + ZERO_STEP, :],
                             zeros[:, :].rearrange("p (o q) -> p o q", o=1).to_broadcast([P, ZERO_STEP, 16 * D]))\
                  .then_inc(rows_zeroed, 16)
            sp.wait_ge(same_made, 2)
            sp.dma_start(same_row.rearrange("(p c) -> p c", p=P), e_half[:, :]).then_inc(same_stored, 16)
            sp.dma_start(restart_row.rearrange("(p c) -> p c", p=P), e_half2[:, :]).then_inc(same_stored, 16)

            for part, data in weight_loads:
                sp.dma_start(part, data).then_inc(weights_in, 16)

            def store_h(v, q):
                sp.wait_ge(h_made[v], q + 1)
                bs = slice(q * NODE_BLOCKS, (q + 1) * NODE_BLOCKS)
                sp.dma_start(table[v].rearrange("(p b) d -> p b d", p=P)[:, bs, :],
                             h[:, bs, 0:widths[v]]).then_inc(h_stored[v], 16)

            for q in range(NQ):
                store_h(0, q)

            sp.wait_ge(carry_made, 1)
            sp.dma_start(carry_dram[0:2, :].rearrange("a p -> p a"), row_stat[:, :],
                         allow_slow_non_contiguous=True).then_inc(carry_hop[0], 16)
            sp.wait_ge(carry_hop[0], 16)
            sp.dma_start(carry_row[:, :, :], carry_dram[0:2, :].rearrange("(o a) p -> o a p", o=1))\
              .then_inc(carry_hop[1], 16)
            sp.wait_ge(carry_made, 2)
            sp.dma_start(carry_dram[2:3, :], carry_scan[0:1, 0:P]).then_inc(carry_hop[2], 16)
            sp.wait_ge(carry_hop[2], 16)
            sp.dma_start(carry[:, :], carry_dram[2:3, :].rearrange("o p -> p o"),
                         allow_slow_non_contiguous=True).then_inc(carry_hop[3], 16)
            sp.wait_ge(ex_made, 1)
            sp.dma_start(ex_row.rearrange("(p c) -> p c", p=P), e_tmp[:, :]).then_inc(ex_stored, 16)
            sp.wait_ge(decay_made, 1)
            sp.dma_start(decay_row.rearrange("(p c) -> p c", p=P), e_max[:, :]).then_inc(ex_stored, 16)

            sp.wait_ge(same_stored, 32)
            sp.wait_ge(ex_stored, 32)
            sp.wait_ge(G_zeroed, 1)
            for l in range(4):
                if l in MLP:
                    sp.wait_ge(h_scattered[l], 16 * B)
                src_view = src_in
                ex_view = ex_row.rearrange("(g c p j) -> g p c j", c=CH, p=P, j=TJ)
                first_view = first_rows[0:E, :].rearrange("(g c p j) d -> g p c j d", c=CH, p=P, j=TJ)
                rows_view = prefix[l].rearrange("(g c p j) d -> g p c (j d)", c=CH, p=P, j=TJ)

                def load(turn, half, l=l, src_view=src_view, ex_view=ex_view, first_view=first_view):
                    g = turn * 2 + half
                    first_turn = isinstance(turn, int) and turn == 0
                    if not first_turn:
                        for s in range(half * CH, (half + 1) * CH):
                            sp.wait_ge(gathered[s], (l * TURNS + turn) * (16 * TJ))
                        sp.sem_inc(sp_passed, 1)
                    sp.dma_start(idx[:, half, :], src_view[bass.ds(g, 1), :, :].rearrange("o p k -> (o p) k"))\
                      .then_inc(idx_in[half], 16)
                    done = turn * RING + (half - 1) * CH
                    if l in MLP:
                        if not first_turn:
                            sp.wait_ge(transposed[l], done)
                            sp.sem_inc(sp_passed, 1)
                        for c in range(CH):
                            sp.dma_start(G[:, half * CH + c, :, 64:112],
                                         first_view[bass.ds(g, 1), :, c, :, :].rearrange("o p j d -> (o p) j d"))\
                              .then_inc(first_in[l][half], 16)
                        if not first_turn:
                            sp.wait_ge(hidden1[l], done)
                            sp.sem_inc(sp_passed, 1)
                        ea = ea0_in if l == 0 else ea3_in
                        ks = K[:, half * CH:(half + 1) * CH, :].rearrange("k c n -> k (c n)")
                        sp.dma_start(ks[48:64, :], ea[0:16, bass.ds(g * GROUP, GROUP)]).then_inc(ea_in[l][half], 16)
                        if l == 0:
                            sp.dma_start(ks[112:128, :], ea[16:32, bass.ds(g * GROUP, GROUP)])\
                              .then_inc(ea_in[l][half], 16)
                    if l == 1:
                        if not first_turn:
                            sp.wait_ge(weighted[l], done)
                            sp.sem_inc(sp_passed, 1)
                        for c in range(CH):
                            sp.dma_start(ex[:, half, c, :],
                                         ex_view[bass.ds(g, 1), :, c, :].rearrange("o p j -> (o p) j"))\
                              .then_inc(ex_in[l][half], 16)
                    if not first_turn:
                        sp.wait_ge(scanned[l], done)
                        sp.sem_inc(sp_passed, 1)
                    rows = P if l in MLP else 64
                    mrow = {0: same_row, 1: decay_row, 2: restart_row, 3: same_row}[l]
                    mdst = mask_f[0:rows, half, :] if l == 1 else mask_h[0:rows, half, 0:GROUP]
                    sp.dma_start(mdst, mrow[bass.ds(g * GROUP, GROUP)].rearrange("(o n) -> o n", o=1)
                                 .to_broadcast([rows, GROUP])).then_inc(mask_in[half], 16)

                def store(turn, half, l=l, rows_view=rows_view):
                    g = turn * 2 + half
                    sp.wait_ge(rows_copied[l], turn * RING + (half + 1) * CH)
                    sp.sem_inc(sp_passed, 1)
                    W = TJ * widths[l]
                    sp.dma_start(rows_view[bass.ds(g, 1), :, :, :].rearrange("o p c w -> (o p) c w"),
                                 O[:, half * CH:(half + 1) * CH, 0:W]).then_inc(rows_stored[half], 16)

                load(0, 0)
                load(0, 1)
                if TURNS > 1:
                    with sp.Fori(1, TURNS) as turn:
                        for half in range(2):
                            load(turn, half)
                            store(turn - 1, half)
                store(TURNS - 1, 0)
                store(TURNS - 1, 1)
                if l < 3:
                    for q in range(NQ):
                        store_h(l + 1, q)
            for q in range(NQ):
                sp.wait_ge(out_made, q + 1)
                bs = slice(q * NODE_BLOCKS, (q + 1) * NODE_BLOCKS)
                sp.dma_start(out.rearrange("(p b) d -> p b d", p=P)[:, bs, :], x[:, bs, :]).then_inc(out_stored, 16)
            sp.wait_ge(out_stored, 16 * NQ)
            for half in range(2):
                sp.wait_ge(rows_stored[half], 16 * TURNS * 4)
            for l in range(4):
                sp.wait_ge(h_stored[l], 16 * NQ)
            for l in MLP:
                sp.wait_ge(h_scattered[l], 16 * B)

        @block.gpsimd
        def _(pool):
            pool.memset(ident[:, :], 0.0).then_inc(ident_set, 1)
            pool.wait_ge(ident_set, 1)
            pool.affine_select(out=ident[:, :], in_=ident[:, :], compare_op=ALU.not_equal, fill=1.0,
                               base=0, pattern=[[-1, P]], channel_multiplier=1).then_inc(ident_done, 1)
            pool.iota(node_id_i[:, :], pattern=[[1, SB]], base=0, channel_multiplier=B).then_inc(node_id_set, 1)
            pool.memset(G[:, :, :, :].rearrange("p a b c -> p (a b c)"), 0.0).then_inc(G_zeroed, 1)
            pool.wait_ge(dstf_stored, 16)
            for r in range(SB // SEARCH_COLS):
                pool.wait_ge(rows_chosen, r + 1)
                if r >= 2:
                    pool.wait_ge(found_used, r - 1)
                for c in range(SEARCH_COLS):
                    b = r * SEARCH_COLS + c
                    pool.indirect_dma_start(found[:, r % 2, c, :], None, dstf,
                                            bass.IndirectOffsetOnAxis(ap=row_i[:, b:b + 1], axis=0))\
                        .then_inc(found_in[r % 2], 16)

            def scatter(v, q):
                pool.wait_ge(h_made[v], q + 1)
                for b in range(q * NODE_BLOCKS, (q + 1) * NODE_BLOCKS):
                    pool.indirect_dma_start(first_rows, bass.IndirectOffsetOnAxis(ap=first_edge[:, b:b + 1], axis=0),
                                            h[:, b, 0:D], None).then_inc(h_scattered[v], 16)

            pool.wait_ge(places_made, 1)
            pool.wait_ge(rows_zeroed, 16 * (EC // 16 // ZERO_STEP))
            for q in range(NQ):
                scatter(0, q)
            pool.wait_ge(G_zeroed, 1)
            for l in range(4):
                pool.wait_ge(h_stored[l], 16 * NQ)

                def gather(c, l=l):
                    if c.at_group_start:
                        pool.wait_ge(idx_in[c.half], (l * TURNS + c.turn + 1) * 16)
                    if not (c.fixed and c.n < RING):
                        pool.wait_ge(transposed[l], c.n - (RING - 1))
                    pool.sem_inc(pool_passed, 1)
                    for j in range(TJ):
                        k = (c.slot % CH) * TJ + j
                        pool.indirect_dma_start(G[:, c.slot, j, 0:widths[l]], None, table[l],
                                                bass.IndirectOffsetOnAxis(ap=idx[:, c.half, k:k + 1], axis=0))\
                            .then_inc(gathered[c.slot], 16)

                pipeline(pool, [(0, gather)], TURNS)
                for half in range(2):
                    pool.wait_ge(rows_stored[half], 16 * TURNS * (l + 1))
                v = l + 1
                for q in range(NQ):
                    if q >= 2:
                        pool.wait_ge(last_rows_used[v], q - 1)
                    for k in range(NODE_BLOCKS):
                        b = q * NODE_BLOCKS + k
                        pool.indirect_dma_start(R[:, q % 2, k, 0:widths[l]], None, prefix[l],
                                                bass.IndirectOffsetOnAxis(ap=last_edge[:, b:b + 1], axis=0))\
                            .then_inc(last_rows_in[v][q % 2], 16)
                    if v == 3 and q:
                        scatter(3, q - 1)
                if v == 3:
                    scatter(3, NQ - 1)

        @block.scalar
        def _(act):
            def sqrt_var(v, q):
                act.wait_ge(var_made[v], q + 1)
                act.activation(ns[:, q % 2, 2, :], ns[:, q % 2, 1, :], ACT.Sqrt, bias=eps[:, :], scale=1.0 / D)\
                   .then_inc(sd_made[v], 1)

            for q in range(NQ):
                sqrt_var(0, q)
            act.wait_ge(ex_arg_made, 1)
            act.activation(e_tmp[:, :], e_tmp[:, :], ACT.Exp).then_inc(ex_made, 1)
            act.wait_ge(ex_arg_made, 2)
            act.activation(e_max[:, :], e_w[:, :], ACT.Exp).then_inc(ex_made, 1)
            act.wait_ge(weights_in, ALL_WEIGHTS)
            for l in range(4):
                def copy_src(c, l=l):
                    act.wait_ge(transposed[l], c.n + 1)
                    if not (c.fixed and c.n < RING):
                        act.wait_ge(hidden1[l], c.n - (RING - 1))
                    act.activation(K[0:D, c.slot, :], pT[c.slot % 2][0:D, :], ACT.Copy).then_inc(src_copied[l], 1)

                def relu_1(c, l=l):
                    act.wait_ge(hidden1[l], c.n + 1)
                    if not (c.fixed and c.n < 4):
                        act.wait_ge(scanned[l] if l == 0 else hidden2[l], c.n - 3)
                    act.activation(H1[:, c.slot % 4, :], pH1[c.slot % 2][:, :], ACT.Relu,
                                   bias=(b1_0 if l == 0 else b1_3)[:, :]).then_inc(relu1[l], 1)

                def relu_2(c, l=l):
                    act.wait_ge(hidden2[l], c.n + 1)
                    if not (c.fixed and c.n < 4):
                        act.wait_ge(scanned[l], c.n - 3)
                    act.activation(H2[:, c.slot % 4, :], pH2[c.slot % 2][:, :], ACT.Relu, bias=b2_3[:, :])\
                       .then_inc(relu2[l], 1)

                def copy_rows(c, l=l):
                    act.wait_ge(rows_made[l], c.n + 1)
                    if c.at_group_start and not (c.fixed and c.n < RING):
                        act.wait_ge(rows_stored[c.half], (l * TURNS + c.turn) * 16)
                    W = TJ * widths[l]
                    act.activation(O[:, c.slot, 0:W], pO[c.slot % 2][:, 0:W], ACT.Copy).then_inc(rows_copied[l], 1)

                stages = {0: [(0, copy_src), (1, relu_1), (3, copy_rows)],
                          1: [(3, copy_rows)],
                          2: [(0, copy_src), (3, copy_rows)],
                          3: [(0, copy_src), (1, relu_1), (3, copy_rows), (1, relu_2)]}[l]
                pipeline(act, stages, TURNS)
                v = l + 1
                for q in range(NQ):
                    if v == 2:
                        act.wait_ge(elu_arg, q + 1)
                        act.activation(u2[:, q % 2, :, :], u2[:, q % 2, :, :], ACT.Exp).then_inc(elu_exp, 1)
                    if v == 3:
                        for i in range(2):
                            act.wait_ge(hT_made, 2 * q + i + 1)
                            if q:
                                act.wait_ge(theta_h, q)
                            act.activation(K[0:D, i, :], pT[i][0:D, :], ACT.Copy).then_inc(hT_copied, 1)
                    if v < 4:
                        sqrt_var(v, q)

        @block.tensor
        def _(pe):
            pe.wait_ge(ident_done, 1)
            pe.wait_ge(G_zeroed, 1)
            pe.wait_ge(weights_in, ALL_WEIGHTS)
            for l in range(4):
                rows_T = 112 if l in MLP else widths[l]

                def transpose_rows(c, l=l, rows_T=rows_T):
                    pe.wait_ge(gathered[c.slot], (l * TURNS + c.turn + 1) * (16 * TJ))
                    if l in MLP and c.at_group_start:
                        pe.wait_ge(first_in[l][c.half], (c.turn + 1) * (16 * CH))
                    if l == 1:
                        pe.wait_ge(weighted[l], c.n + 1)
                    if not (c.fixed and c.n < 2):
                        if l in MLP:
                            pe.wait_ge(dst_spread[l], c.n - 1)
                        if l != 1:
                            pe.wait_ge(src_copied[l], c.n - 1)
                        else:
                            pe.wait_ge(scanned[l], c.n - 1)
                    pe.sem_inc(pe_passed, 1)
                    o = pT[c.slot % 2][:, :].rearrange("k (p j) -> k p j", j=TJ)
                    for j in range(TJ):
                        last = pe.transpose(o[0:rows_T, :, j], G[:, c.slot, j, 0:rows_T], ident[:, :])
                    last.then_inc(transposed[l], 1)

                def layer_1(c, l=l):
                    pe.wait_ge(src_copied[l], c.n + 1)
                    if l in MLP:
                        pe.wait_ge(dst_spread[l], c.n + 1)
                        if c.at_group_start:
                            pe.wait_ge(ea_in[l][c.half], (c.turn + 1) * (32 if l == 0 else 16))
                    if not (c.fixed and c.n < 2):
                        pe.wait_ge(relu1[l] if l in MLP else scanned[l], c.n - 1)
                    if l in MLP:
                        k = KROWS[l]
                        w = w1_0 if l == 0 else w1_3
                        pe.matmul(pH1[c.slot % 2][:, :], w[0:k, :], K[0:k, c.slot, :], start=True, stop=True)\
                          .then_inc(hidden1[l], 1)
                    else:
                        pe.sem_inc(pe_passed, 1)
                        pe.matmul(pH1[c.slot % 2][0:D, :], wq[:, :], K[0:D, c.slot, :], start=True, stop=True)\
                          .then_inc(hidden1[l], 1)

                def layer_2(c, l=l):
                    pe.wait_ge(relu1[l], c.n + 1)
                    if not (c.fixed and c.n < 2):
                        pe.wait_ge(relu2[l], c.n - 1)
                    pe.matmul(pH2[c.slot % 2][:, :], w2_3[:, :], H1[:, c.slot % 4, :], start=True, stop=True)\
                      .then_inc(hidden2[l], 1)

                def make_rows(c, l=l):
                    pe.wait_ge(scanned[l], c.n + 1)
                    if not (c.fixed and c.n < 2):
                        pe.wait_ge(rows_copied[l], c.n - 1)
                    pe.sem_inc(pe_passed, 1)
                    w = widths[l]
                    s = S[:, c.slot % 4, :].rearrange("k (p j) -> k p j", j=TJ)
                    for j in range(TJ):
                        o = pO[c.slot % 2][:, j * w:(j + 1) * w]
                        if l in MLP:
                            last = pe.matmul(o, s[:, :, j], (w2_0 if l == 0 else w3_3)[:, :], start=True, stop=True)
                        else:
                            last = pe.transpose(o, s[0:w, :, j], ident[0:w, 0:w])
                    last.then_inc(rows_made[l], 1)

                if l == 2:
                    pe.wait_ge(wq_made, 1)
                stages = {0: [(0, transpose_rows), (1, layer_1), (3, make_rows)],
                          1: [(0, transpose_rows), (3, make_rows)],
                          2: [(0, transpose_rows), (1, layer_1), (3, make_rows)],
                          3: [(0, transpose_rows), (1, layer_1), (3, make_rows), (1, layer_2)]}[l]
                pipeline(pe, stages, TURNS)
                if l == 2:
                    pe.wait_ge(src_copied[2], NCH)
                    pe.wait_ge(rows_copied[2], NCH)
                    for q in range(NQ):
                        for i in range(2):
                            if q:
                                pe.wait_ge(hT_copied, 2 * (q - 1) + i + 1)
                            ks = range(i * 4, min(NODE_BLOCKS, i * 4 + 4))
                            for k in ks:
                                last = pe.transpose(pT[i][0:D, (k - 4 * i) * P:(k - 4 * i + 1) * P],
                                                    h[:, q * NODE_BLOCKS + k, 0:D], ident[:, :])
                            last.then_inc(hT_made, 1)
                        pe.wait_ge(hT_copied, 2 * q + 2)
                        if q >= 2:
                            pe.wait_ge(last_rows_used[3], q - 1)
                        for k in range(NODE_BLOCKS):
                            last = pe.matmul(pO[q % 2][:, k * D:(k + 1) * D],
                                             K[0:D, k // 4, (k % 4) * P:(k % 4 + 1) * P], thetaT[:, :],
                                             start=True, stop=True)
                        last.then_inc(theta_h, 1)

        @block.vector
        def _(dve):
            own = [0]

            def link(ins):
                own[0] += 1
                ins.then_inc(vector_done, 1)
                dve.wait_ge(vector_done, own[0])

            link(dve.memset(zeros[:, :], 0.0))
            dve.memset(zeros[:, 0:1], 0.0).then_inc(zeros_set, 1)
            link(dve.memset(eps[:, :], 1e-5))
            link(dve.memset(h[:, :, D:D + 1], 1.0))
            link(dve.memset(K[:, RING - 1, CHUNK - 1:CHUNK], 0.0))
            link(dve.memset(S[:, 3, CHUNK - 1:CHUNK], 0.0))
            dve.wait_ge(edges_in, 32)
            dve.tensor_copy(e_tmp[:, :], e_dst[:, :]).then_inc(dstf_made, 1)
            link(dve.tensor_tensor(e_start[:, :], e_dst[:, :], e_prev[:, :], ALU.not_equal))
            dve.tensor_scalar(e_half[:, :], e_start[:, :], -1.0, 1.0, ALU.mult, ALU.add).then_inc(same_made, 1)
            dve.tensor_scalar(e_half2[:, :], e_start[:, :], -BIG, None, ALU.mult).then_inc(same_made, 1)

            dve.wait_ge(heads_loaded, 16)
            dve.wait_ge(node_id_set, 1)
            link(dve.tensor_copy(heads[:, :], heads_i[:, :]))
            link(dve.tensor_copy(node_id[:, :], node_id_i[:, :]))

            def choose_rows(r):
                cs = slice(r * SEARCH_COLS, (r + 1) * SEARCH_COLS)
                for b in range(cs.start, cs.stop):
                    link(dve.tensor_scalar(below[:, 0:ROWS], heads[:, :], node_id[:, b:b + 1], None,
                                           ALU.is_lt, ALU.add, accum_out=heads_below[:, b:b + 1]))
                link(dve.tensor_scalar(row_f[:, cs], heads_below[:, cs], -1.0, 0.0, ALU.add, ALU.max))
                dve.tensor_copy(row_i[:, cs], row_f[:, cs]).then_inc(rows_chosen, 1)

            def count_in_rows(r):
                dve.wait_ge(found_in[r % 2], (r // 2 + 1) * 16 * SEARCH_COLS)
                for c in range(SEARCH_COLS):
                    b = r * SEARCH_COLS + c
                    link(dve.tensor_scalar(below[:, ROWS:ROWS + COLS], found[:, r % 2, c, :], node_id[:, b:b + 1],
                                           None, ALU.is_lt, ALU.add, accum_out=in_row[:, b:b + 1]))
                dve.tensor_copy(ns[:, 0, 0, 0:1], in_row[:, b:b + 1]).then_inc(found_used, 1)

            rounds = SB // SEARCH_COLS
            for r in range(rounds + 2):
                if r < rounds:
                    choose_rows(r)
                if r == 1:
                    dve.wait_ge(x_loaded, 16)
                if r >= 2:
                    count_in_rows(r - 2)
            dve.wait_ge(found_used, rounds)
            link(dve.scalar_tensor_tensor(start[:, :], row_f[:, :], float(COLS), in_row[:, :], ALU.mult, ALU.add))
            link(dve.tensor_tensor(count[:, :], start[:, 1:B + 1], start[:, 0:B], ALU.subtract))
            link(dve.tensor_scalar(filled[:, :], count[:, :], 0.0, None, ALU.is_gt))
            link(dve.tensor_scalar(empty[:, :], filled[:, :], -1.0, 1.0, ALU.mult, ALU.add))
            link(dve.tensor_scalar(last_edge[:, :], start[:, 1:B + 1], -1.0, 0.0, ALU.add, ALU.max))
            link(dve.tensor_scalar(node_tmp[:, :], count[:, :], 1.0, None, ALU.max))
            link(dve.reciprocal(inv_count[:, :], node_tmp[:, :]))
            link(dve.tensor_scalar(node_tmp[:, :], node_id[:, 0:B], float(E), None, ALU.add))
            link(dve.tensor_tensor(node_id[:, 0:B], start[:, 0:B], node_tmp[:, :], ALU.subtract))
            link(dve.tensor_tensor(node_id[:, 0:B], node_id[:, 0:B], filled[:, :], ALU.mult))
            dve.tensor_tensor(first_edge[:, :], node_id[:, 0:B], node_tmp[:, :], ALU.add).then_inc(places_made, 1)

            def over_features(v):
                return v.rearrange("p (b o) -> p b o", o=1).to_broadcast([P, NODE_BLOCKS, D])

            def layernorm(v, q):
                bs = slice(q * NODE_BLOCKS, (q + 1) * NODE_BLOCKS)
                s = q % 2
                link(dve.tensor_reduce(ns[:, s, 0, :], x[:, bs, :], AX, ALU.add))
                link(dve.tensor_scalar(ns[:, s, 0, :], ns[:, s, 0, :], 1.0 / D, None, ALU.mult))
                link(dve.tensor_tensor(u[:, s, :, :], x[:, bs, :], over_features(ns[:, s, 0, :]), ALU.subtract))
                link(dve.tensor_tensor(u2[:, s, :, :], u[:, s, :, :], u[:, s, :, :], ALU.mult))
                dve.tensor_reduce(ns[:, s, 1, :], u2[:, s, :, :], AX, ALU.add).then_inc(var_made[v], 1)

            def finish_norm(v, q):
                bs = slice(q * NODE_BLOCKS, (q + 1) * NODE_BLOCKS)
                s = q % 2
                dve.wait_ge(sd_made[v], q + 1)
                link(dve.reciprocal(ns[:, s, 3, :], ns[:, s, 2, :]))
                dve.scalar_tensor_tensor(h[:, bs, 0:D], u[:, s, :, :], 0.0, over_features(ns[:, s, 3, :]),
                                         ALU.max, ALU.mult).then_inc(h_made[v], 1)

            for q in range(NQ):
                layernorm(0, q)
                if q:
                    finish_norm(0, q - 1)
            finish_norm(0, NQ - 1)

            dve.wait_ge(w_edge_in, 16)
            dve.wait_ge(dstf_stored, 16)
            link(dve.tensor_scalar(e_tmp[:, :], e_start[:, :], -BIG, None, ALU.mult))
            link(dve.tensor_tensor_scan(e_max[:, :], e_tmp[:, :], e_w[:, :], -BIG, ALU.add, ALU.max))
            link(dve.tensor_copy(row_stat[:, 1:2], e_max[:, EC - 1:EC]))
            dve.tensor_reduce(row_stat[:, 0:1], e_tmp[:, :], AX, ALU.min).then_inc(carry_made, 1)
            link(dve.memset(carry_scan[:, 0:1], -BIG))
            dve.wait_ge(carry_hop[1], 16)
            dve.tensor_tensor_scan(carry_scan[:, 1:P + 1], carry_row[:, 0, :], carry_row[:, 1, :], -BIG,
                                   ALU.add, ALU.max).then_inc(carry_made, 1)
            dve.wait_ge(carry_hop[3], 16)
            link(dve.tensor_tensor_scan(e_max[:, :], e_tmp[:, :], e_w[:, :], carry[:, :], ALU.add, ALU.max))
            dve.tensor_tensor(e_tmp[:, :], e_w[:, :], e_max[:, :], ALU.subtract).then_inc(ex_arg_made, 1)
            link(dve.tensor_copy(row_stat[:, 0:1], carry[:, :]))
            dve.wait_ge(ex_made, 1)
            link(dve.tensor_tensor(e_w[:, 1:EC], e_max[:, 0:EC - 1], e_max[:, 1:EC], ALU.subtract))
            link(dve.tensor_tensor(e_w[:, 0:1], carry[:, :], e_max[:, 0:1], ALU.subtract))
            dve.tensor_scalar(e_w[:, :], e_w[:, :], 0.0, None, ALU.min).then_inc(ex_arg_made, 1)
            dve.wait_ge(ex_made, 2)
            link(dve.tensor_scalar(e_start[:, :], e_start[:, :], -1.0, 1.0, ALU.mult, ALU.add))
            dve.tensor_tensor(e_max[:, :], e_max[:, :], e_start[:, :], ALU.mult).then_inc(decay_made, 1)

            dve.wait_ge(weights_in, ALL_WEIGHTS)
            dve.tensor_tensor(wq[:, :], phiT[:, :], thetaT[:, :], ALU.subtract).then_inc(wq_made, 1)
            link(dve.tensor_tensor(tb[:, :, :], tb[:, :, :], pb[:, :, :], ALU.add))

            for l in range(4):
                def weight_rows(c, l=l):
                    dve.wait_ge(gathered[c.slot], (l * TURNS + c.turn + 1) * (16 * TJ))
                    if c.at_group_start:
                        dve.wait_ge(ex_in[l][c.half], (c.turn + 1) * (16 * CH))
                    g = G[:, c.slot, :, 0:D + 1]
                    e = ex[:, c.half, c.slot % CH, :].rearrange("p (j o) -> p j o", o=1).to_broadcast([P, TJ, D + 1])
                    dve.tensor_tensor(g, g, e, ALU.mult).then_inc(weighted[l], 1)

                def mask_of(c, rows, l=l):
                    m = mask_f if l == 1 else mask_h
                    k = c.slot % CH
                    return m[rows, c.half, k * CHUNK:(k + 1) * CHUNK]

                def spread_dst(c, l=l):
                    if c.at_group_start:
                        dve.wait_ge(mask_in[c.half], (l * TURNS + c.turn + 1) * 16)
                    dve.wait_ge(transposed[l], c.n + 1)
                    if not (c.fixed and c.n == 0):
                        dve.wait_ge(dst_spread[l], c.n)
                    if not (c.fixed and c.n < RING):
                        dve.wait_ge(hidden1[l], c.n - (RING - 1))
                    r = slice(64, 112)
                    dve.tensor_tensor_scan(K[r, c.slot, :], mask_of(c, r), pT[c.slot % 2][r, :],
                                           K[r, (c.slot - 1) % RING, CHUNK - 1:CHUNK], ALU.mult, ALU.add)\
                       .then_inc(dst_spread[l], 1)

                def scan(c, l=l):
                    if l not in MLP and c.at_group_start:
                        dve.wait_ge(mask_in[c.half], (l * TURNS + c.turn + 1) * 16)
                    dve.wait_ge({0: relu1, 1: transposed, 2: hidden1, 3: relu2}[l][l], c.n + 1)
                    if not (c.fixed and c.n == 0):
                        dve.wait_ge(scanned[l], c.n)
                    if not (c.fixed and c.n < 4):
                        dve.wait_ge(rows_made[l], c.n - 3)
                    r = slice(0, P if l in MLP else widths[l])
                    data = {0: H1[:, c.slot % 4, :], 1: pT[c.slot % 2][r, :], 2: pH1[c.slot % 2][r, :],
                            3: H2[:, c.slot % 4, :]}[l]
                    op0, op1 = (ALU.add, ALU.max) if l == 2 else (ALU.mult, ALU.add)
                    dve.tensor_tensor_scan(S[r, c.slot % 4, :], mask_of(c, r), data,
                                           S[r, (c.slot - 1) % 4, CHUNK - 1:CHUNK], op0, op1)\
                       .then_inc(scanned[l], 1)

                stages = {0: [(0, spread_dst), (2, scan)],
                          1: [(0, weight_rows), (1, scan)],
                          2: [(2, scan)],
                          3: [(0, spread_dst), (2, scan)]}[l]
                pipeline(dve, stages, TURNS)

                v = l + 1
                for q in range(NQ + 1):
                    if v < 4 and q:
                        finish_norm(v, q - 1)
                    if q == NQ:
                        break
                    s = q % 2
                    bs = slice(q * NODE_BLOCKS, (q + 1) * NODE_BLOCKS)
                    rows = R[:, s, :, 0:D]
                    dve.wait_ge(last_rows_in[v][s], (q // 2 + 1) * 16 * NODE_BLOCKS)
                    if v == 1:
                        link(dve.tensor_tensor(u[:, s, :, :], rows, over_features(filled[:, bs]), ALU.mult))
                        link(dve.tensor_tensor(x[:, bs, :], x[:, bs, :], u[:, s, :, :], ALU.add))
                        link(dve.tensor_tensor(u2[:, s, :, :], over_features(count[:, bs]),
                                               b2_0[:, :, :].to_broadcast([P, NODE_BLOCKS, D]), ALU.mult))
                        dve.tensor_tensor(x[:, bs, :], x[:, bs, :], u2[:, s, :, :], ALU.add)\
                           .then_inc(last_rows_used[v], 1)
                        dve.wait_ge(last_rows_used[v], q + 1)
                    elif v == 2:
                        den = ns[:, s, 4, :]
                        link(dve.tensor_tensor(den, R[:, s, :, D], filled[:, bs], ALU.mult))
                        link(dve.tensor_tensor(den, den, empty[:, bs], ALU.add))
                        link(dve.reciprocal(ns[:, s, 5, :], den))
                        link(dve.tensor_tensor(ns[:, s, 5, :], ns[:, s, 5, :], filled[:, bs], ALU.mult))
                        link(dve.tensor_tensor(u[:, s, :, :], rows, over_features(ns[:, s, 5, :]), ALU.mult))
                        dve.tensor_scalar(u2[:, s, :, :], u[:, s, :, :], 0.0, None, ALU.min).then_inc(elu_arg, 1)
                        dve.wait_ge(elu_exp, q + 1)
                        link(dve.scalar_tensor_tensor(u[:, s, :, :], u[:, s, :, :], 0.0, u2[:, s, :, :],
                                                      ALU.max, ALU.add))
                        dve.scalar_tensor_tensor(x[:, bs, :], u[:, s, :, :], -1.0, x[:, bs, :], ALU.add, ALU.add)\
                           .then_inc(last_rows_used[v], 1)
                        dve.wait_ge(last_rows_used[v], q + 1)
                    elif v == 3:
                        dve.wait_ge(theta_h, q + 1)
                        link(dve.tensor_tensor(u[:, s, :, :], rows,
                                               pO[s][:, 0:NODE_BLOCKS * D].rearrange("p (b d) -> p b d", d=D), ALU.add))
                        link(dve.tensor_tensor(u[:, s, :, :], u[:, s, :, :],
                                               tb[:, :, :].to_broadcast([P, NODE_BLOCKS, D]), ALU.add))
                        link(dve.tensor_tensor(u[:, s, :, :], u[:, s, :, :], over_features(filled[:, bs]), ALU.mult))
                        dve.tensor_tensor(x[:, bs, :], x[:, bs, :], u[:, s, :, :], ALU.add)\
                           .then_inc(last_rows_used[v], 1)
                        dve.wait_ge(last_rows_used[v], q + 1)
                    else:
                        link(dve.tensor_tensor(u[:, s, :, :], rows, over_features(inv_count[:, bs]), ALU.mult))
                        link(dve.tensor_tensor(u[:, s, :, :], u[:, s, :, :],
                                               b3_3[:, :, :].to_broadcast([P, NODE_BLOCKS, D]), ALU.add))
                        dve.tensor_tensor(u[:, s, :, :], u[:, s, :, :], over_features(filled[:, bs]), ALU.mult)\
                           .then_inc(last_rows_used[v], 1)
                        dve.wait_ge(last_rows_used[v], q + 1)
                        link(dve.tensor_tensor(u[:, s, :, :], u[:, s, :, :], h[:, bs, 0:D], ALU.add))
                        dve.tensor_tensor(x[:, bs, :], x[:, bs, :], u[:, s, :, :], ALU.add).then_inc(out_made, 1)
                    if v < 4:
                        layernorm(v, q)


def kernel(**inputs):
    import numpy as np
    import concourse.bacc as _bacc
    from concourse import mybir as _mybir
    from concourse.bass_utils import run_bass_kernel_spmd as _run

    x = np.asarray(inputs["x"])
    n_nodes = x.shape[0]
    blocks = -(-n_nodes // (P * NODE_BLOCKS)) * NODE_BLOCKS
    N = P * blocks
    assert N > n_nodes
    edges = np.asarray(inputs["src"]).shape[0]
    E = -(-edges // (2 * GROUP)) * 2 * GROUP
    rows = max(r for r in range(1, int(E ** 0.5) + 1) if E % r == 0)

    def padded(a, fill):
        a = np.asarray(a)
        return np.concatenate([a, np.full((E - edges,) + a.shape[1:], fill, a.dtype)])

    src = padded(inputs["src"], 0)
    dst = padded(inputs["dst"], n_nodes)
    arrays = {
        "x": np.concatenate([x, np.zeros((N - n_nodes, D), x.dtype)]),
        "src": np.ascontiguousarray(src.reshape(-1, CH, P, TJ).transpose(0, 2, 1, 3)).reshape(-1, P, CH * TJ),
        "dst": dst,
        "dst_prev": np.concatenate([np.full((1,), -1, dst.dtype), dst[:-1]]),
        "heads": np.ascontiguousarray(dst.reshape(rows, -1)[:, 0]),
        "ea0": np.ascontiguousarray(padded(inputs["edge_attr_32"], 0).T),
        "ea3": np.ascontiguousarray(padded(inputs["edge_attr_16"], 0).T),
        "w": padded(inputs["edge_weight1"], 0)[:, 0],
        "L0_W1": inputs["L0_gnn_W1"], "L0_b1": inputs["L0_gnn_b1"],
        "L0_W2": inputs["L0_gnn_W2"], "L0_b2": inputs["L0_gnn_b2"],
        "thetaT": np.asarray(inputs["L2_gnn_theta_w"]).T, "phiT": np.asarray(inputs["L2_gnn_phi_w"]).T,
        "theta_b": inputs["L2_gnn_theta_b"], "phi_b": inputs["L2_gnn_phi_b"],
        "L3_W1": inputs["L3_gnn_W1"], "L3_b1": inputs["L3_gnn_b1"],
        "L3_W2": inputs["L3_gnn_W2"], "L3_b2": inputs["L3_gnn_b2"],
        "L3_W3": inputs["L3_gnn_W3"], "L3_b3": inputs["L3_gnn_b3"],
    }
    nc = _bacc.Bacc("TRN2", target_bir_lowering=False, num_devices=1)
    given, args = {}, []
    for name, a in arrays.items():
        a = np.ascontiguousarray(a)
        given[f"in_{name}_dram"] = a
        args.append(nc.dram_tensor(f"in_{name}_dram", a.shape, _mybir.dt.from_np(a.dtype), kind="ExternalInput").ap())
    args.append(nc.dram_tensor("out_dram", (N, D), _mybir.dt.float32, kind="ExternalOutput").ap())
    build(nc, *args)
    r = _run(nc, [given], core_ids=[0])
    return r.results[0]["out_dram"][:n_nodes]
```

```python
import concourse.bass as bass
from concourse import mybir
from contextlib import ExitStack

P = 128
D = 48
TJ = 4
CHUNK = P * TJ
CH = 4
GROUP = CH * CHUNK
RING = 2 * CH
NODE_BLOCKS = 7
COUNT_COLS = 32
BIG = 3.0e38


class Chunk:

    def __init__(self, turn, k):
        self.slot = k % RING
        self.turn = turn + k // RING
        self.n = turn * RING + k
        self.half = self.slot // CH
        self.at_group_start = self.slot % CH == 0
        self.fixed = isinstance(self.n, int)


def pipeline(eng, stages, turns, loop_turns=None):
    loop_turns = turns if loop_turns is None else loop_turns
    for k in range(RING):
        for lag, stage in stages:
            if k >= lag:
                stage(Chunk(0, k - lag))
    if loop_turns > 1:
        with eng.Fori(1, loop_turns) as turn:
            for k in range(RING):
                for lag, stage in stages:
                    stage(Chunk(turn, k - lag))
    for turn in range(max(loop_turns, 1), turns):
        for k in range(RING):
            for lag, stage in stages:
                stage(Chunk(turn, k - lag))
    for k in range(max(lag for lag, _ in stages)):
        for lag, stage in stages:
            if k < lag:
                stage(Chunk(turns, k - lag))


def build(nc, x_in, src_in, dst_in, dst_prev_in, ea0_in, ea3_in, w_in,
          L0_W1, L0_b1, L0_W2, L0_b2, thetaT_in, phiT_in, theta_b, phi_b,
          L3_W1, L3_b1, L3_W2, L3_b2, L3_W3, L3_b3, out):
    f32, i32, bf16 = mybir.dt.float32, mybir.dt.int32, mybir.dt.bfloat16
    ALU = mybir.AluOpType
    ACT = mybir.ActivationFunctionType
    AX = mybir.AxisListType.X

    N = x_in.shape[0]
    B = N // P
    E = dst_in.shape[0]
    EC = E // P
    LO = P
    HI = N // LO
    GROUPS = E // GROUP
    TURNS = GROUPS // 2
    NCH = E // CHUNK
    NQ = B // NODE_BLOCKS
    SPLIT = max(1, TURNS * 3 // 8)
    HID = L0_W1.shape[1]
    ZERO_STEP = next(k for k in (7, 6, 5, 3, 2, 1) if EC // 16 % k == 0)
    assert B % NODE_BLOCKS == 0 and GROUPS % 2 == 0 and NCH % RING == 0

    dram = lambda name, shape, dt: nc.dram_tensor(name, shape, dt, kind="Internal").ap()
    widths = [D, D + 1, D, D]
    table = [dram(f"table{l}", (N, widths[l]), f32) for l in range(4)]
    prefix = [dram(f"prefix{l}", (E, widths[l]), f32) for l in range(4)]
    first_rows = dram("first_rows", (E + N, D), f32)
    spool = dram("spool", (E, D), f32)
    count_dram = dram("count_dram", (2, N), f32)
    same_row = dram("same_row", (E,), bf16)
    restart_row = dram("restart_row", (E,), bf16)
    decay_row = dram("decay_row", (E,), f32)
    ex_row = dram("ex_row", (E,), f32)
    carry_dram = dram("carry_dram", (3, P), f32)

    ctx = ExitStack()
    with ctx:
        def sb(name, shape, dt=f32):
            return ctx.enter_context(nc.sbuf_tensor(name, shape, dt))

        def sem(name):
            return ctx.enter_context(nc.semaphore(name))

        x = sb("x", [P, B, D])
        h = sb("h", [P, B, D + 1])
        end = sb("end", [P, B])
        count = sb("count", [P, B])
        filled = sb("filled", [P, B])
        empty = sb("empty", [P, B])
        inv_count = sb("inv_count", [P, B])
        last_edge = sb("last_edge", [P, B], i32)
        first_edge = sb("first_edge", [P, B], i32)
        node_tmp = sb("node_tmp", [P, B])
        ident = sb("ident", [P, P])
        w1_0 = sb("w1_0", [P, HID])
        w1_3 = sb("w1_3", [P, HID])
        w2_0 = sb("w2_0", [P, D])
        w2_3 = sb("w2_3", [P, HID])
        w3_3 = sb("w3_3", [P, D])
        thetaT = sb("thetaT", [D, D])
        phiT = sb("phiT", [D, D])
        wq = sb("wq", [D, D])
        b1_0 = sb("b1_0", [P, 1])
        b1_3 = sb("b1_3", [P, 1])
        b2_3 = sb("b2_3", [P, 1])
        b2_0 = sb("b2_0", [P, 1, D])
        b3_3 = sb("b3_3", [P, 1, D])
        tb = sb("tb", [P, 1, D])
        pb = sb("pb", [P, 1, D])
        eps = sb("eps", [P, 1])
        zeros = sb("zeros", [P, 16 * D])
        e_dst = sb("e_dst", [P, EC], i32)
        e_prev = sb("e_prev", [P, EC], i32)
        e_w = sb("e_w", [P, EC])
        e_start = sb("e_start", [P, EC])
        e_max = sb("e_max", [P, EC])
        e_tmp = sb("e_tmp", [P, EC])
        e_half = sb("e_half", [P, EC], bf16)
        e_half2 = sb("e_half2", [P, EC], bf16)
        row_stat = sb("row_stat", [P, 2])
        carry_row = sb("carry_row", [1, 2, P])
        carry_scan = sb("carry_scan", [1, P + 1])
        carry = sb("carry", [P, 1])
        low_ids_i = sb("low_ids_i", [P, LO], i32)
        low_ids = sb("low_ids", [P, LO], bf16)[:, :]
        high_cols = sb("high_cols", [P, COUNT_COLS])
        low_cols = sb("low_cols", [P, COUNT_COLS])
        high_hot = sb("high_hot", [P, COUNT_COLS, LO], bf16)
        low_hot = sb("low_hot", [P, COUNT_COLS, LO], bf16)
        counts = sb("counts", [HI, 2, LO])
        row_total = sb("row_total", [HI, 1])
        above = sb("above", [P, P])
        node_id_i = sb("node_id_i", [P, B], i32)
        node_id = sb("node_id", [P, B])
        idx = sb("idx", [P, 2, CH * TJ], i32)
        Gs = sb("Gs", [P, RING, TJ * D])
        G = sb("G", [P, RING, TJ, 112])
        K = sb("K", [P, RING, CHUNK])
        H1 = sb("H1", [P, 4, CHUNK])
        S = sb("S", [P, 4, CHUNK])
        O = sb("O", [P, RING, TJ * (D + 1)])
        mask_f = sb("mask_f", [P, 2, GROUP])
        mask_h = mask_f[:, :, :].bitcast(bf16)
        ex = sb("ex", [P, 2, CH, TJ])
        R = sb("R", [P, 2, NODE_BLOCKS, D + 1])
        u = sb("u", [P, 2, NODE_BLOCKS, D])
        u2 = sb("u2", [P, 2, NODE_BLOCKS, D])
        ns = sb("ns", [P, 2, 6, NODE_BLOCKS])

        pT = [ctx.enter_context(nc.psum_tensor(f"pT{i}", [P, CHUNK], f32)) for i in range(2)]
        pH1 = [ctx.enter_context(nc.psum_tensor(f"pH1_{i}", [P, CHUNK], f32)) for i in range(2)]
        pH2 = [ctx.enter_context(nc.psum_tensor(f"pH2_{i}", [P, CHUNK], f32)) for i in range(2)]
        pO = [ctx.enter_context(nc.psum_tensor(f"pO{i}", [P, CHUNK], f32)) for i in range(2)]

        weights_in = sem("weights_in")
        edges_in = sem("edges_in")
        w_edge_in = sem("w_edge_in")
        x_loaded = [sem(f"x_loaded{i}") for i in range(2)]
        zeros_set = sem("zeros_set")
        rows_zeroed = sem("rows_zeroed")
        ident_set = sem("ident_set")
        ident_done = sem("ident_done")
        node_id_set = sem("node_id_set")
        G_zeroed = sem("G_zeroed")
        cols_copied = sem("cols_copied")
        hot_made = sem("hot_made")
        hot_counted = sem("hot_counted")
        totals_made = sem("totals_made")
        totals_summed = sem("totals_summed")
        ends_made = sem("ends_made")
        ends_stored = sem("ends_stored")
        ends_in = sem("ends_in")
        same_made = sem("same_made")
        same_stored = sem("same_stored")
        carry_made = sem("carry_made")
        carry_hop = [sem(f"carry_hop{i}") for i in range(4)]
        ex_arg_made = sem("ex_arg_made")
        ex_made = sem("ex_made")
        decay_made = sem("decay_made")
        ex_stored = sem("ex_stored")
        places_made = sem("places_made")
        vector_done = sem("vector_done")
        wq_made = sem("wq_made")
        sp_passed = sem("sp_passed")
        act_passed = sem("act_passed")
        dve_passed = sem("dve_passed")
        pool_passed = sem("pool_passed")
        pe_passed = sem("pe_passed")
        out_made = sem("out_made")
        out_stored = sem("out_stored")
        last_rows_in = {v: [sem(f"last_rows_in{v}_{i}") for i in range(2)] for v in range(1, 5)}
        last_rows_used = {v: sem(f"last_rows_used{v}") for v in range(1, 5)}
        elu_arg = sem("elu_arg")
        elu_exp = sem("elu_exp")
        var_made = [sem(f"var_made{v}") for v in range(4)]
        sd_made = [sem(f"sd_made{v}") for v in range(4)]
        h_made = [sem(f"h_made{v}") for v in range(4)]
        h_stored = [sem(f"h_stored{v}") for v in range(4)]
        h_scattered = {v: sem(f"h_scattered{v}") for v in (0, 3)}
        hT_made = sem("hT_made")
        hT_copied = sem("hT_copied")
        theta_h = sem("theta_h")
        def per_layer(name, layers=(0, 1, 2, 3)):
            return {l: sem(f"{name}{l}") for l in layers}

        def per_half(name, layers):
            return {l: [sem(f"{name}{l}_{i}") for i in range(2)] for l in layers}

        MLP = (0, 3)
        idx_in = [sem(f"idx_in{i}") for i in range(2)]
        spool_stored = [sem(f"spool_stored{i}") for i in range(2)]
        rows_in = [sem(f"rows_in{i}") for i in range(RING // 2)]
        first_in = per_half("first_in", (3,))
        mask_in = [sem(f"mask_in{i}") for i in range(2)]
        ea_in = per_half("ea_in", MLP)
        ex_in = per_half("ex_in", (1,))
        gathered = [sem(f"gathered{i}") for i in range(RING)]
        weighted = per_layer("weighted", (1,))
        transposed = per_layer("transposed")
        src_copied = per_layer("src_copied", (0, 2, 3))
        dst_spread = per_layer("dst_spread", MLP)
        hidden1 = per_layer("hidden1_", (0, 2, 3))
        relu1 = per_layer("relu1_", MLP)
        hidden2 = per_layer("hidden2_", (3,))
        relu2 = per_layer("relu2_", (3,))
        scanned = per_layer("scanned")
        rows_made = per_layer("rows_made")
        rows_copied = per_layer("rows_copied")
        rows_stored = [sem(f"rows_stored{i}") for i in range(2)]

        KROWS = {0: 128, 3: 112}
        def column(v):
            return v.rearrange("(h o) -> h o", o=1)

        def on_all(v):
            return v.rearrange("(o d) -> o d", o=1).to_broadcast([P, D])

        weight_loads = [
            (w1_0[0:48, :], L0_W1[0:48, :]), (w1_0[48:64, :], L0_W1[96:112, :]),
            (w1_0[64:112, :], L0_W1[48:96, :]), (w1_0[112:128, :], L0_W1[112:128, :]),
            (w1_3[0:48, :], L3_W1[0:48, :]), (w1_3[48:64, :], L3_W1[96:112, :]),
            (w1_3[64:112, :], L3_W1[48:96, :]),
            (w2_0[:, :], L0_W2), (w2_3[:, :], L3_W2), (w3_3[:, :], L3_W3),
            (thetaT[:, :], thetaT_in), (phiT[:, :], phiT_in),
            (b1_0[:, :], column(L0_b1)), (b1_3[:, :], column(L3_b1)), (b2_3[:, :], column(L3_b2)),
            (b2_0[:, 0, :], on_all(L0_b2)), (b3_3[:, 0, :], on_all(L3_b3)),
            (tb[:, 0, :], on_all(theta_b)), (pb[:, 0, :], on_all(phi_b)),
        ]
        ALL_WEIGHTS = 16 * len(weight_loads)

        first_view = first_rows[0:E, :].rearrange("(g c p j) d -> g p c j d", c=CH, p=P, j=TJ)
        spool_view = spool.rearrange("(g c p j) d -> g p c (j d)", c=CH, p=P, j=TJ)
        first_flat = first_rows[0:E, :].rearrange("(g c p j) d -> g p c (j d)", c=CH, p=P, j=TJ)
        G0 = G[:, :, :, :].rearrange("p s j w -> p s (j w)")

        block = ctx.enter_context(nc.Block())

        @block.sync
        def _(sp):
            x_view = x_in.rearrange("(p b) d -> p b d", p=P)
            for n, bs in enumerate((slice(0, NODE_BLOCKS), slice(NODE_BLOCKS, B))):
                if bs.start < bs.stop:
                    sp.dma_start(x[:, bs, :], x_view[:, bs, :]).then_inc(x_loaded[n], 16)
            sp.dma_start(e_dst[:, :], dst_in.rearrange("(p c) -> p c", p=P)).then_inc(edges_in, 16)
            sp.dma_start(e_prev[:, :], dst_prev_in.rearrange("(p c) -> p c", p=P)).then_inc(edges_in, 16)

            def store_h(v, q):
                sp.wait_ge(h_made[v], q + 1)
                bs = slice(q * NODE_BLOCKS, (q + 1) * NODE_BLOCKS)
                sp.dma_start(table[v].rearrange("(p b) d -> p b d", p=P)[:, bs, :],
                             h[:, bs, 0:widths[v]]).then_inc(h_stored[v], 16)

            for q in range(NQ):
                store_h(0, q)

            def idx_load(turn, half):
                g = turn * 2 + half
                sp.dma_start(idx[:, half, :], src_in[bass.ds(g, 1), :, :].rearrange("o p k -> (o p) k"))\
                  .then_inc(idx_in[half], 16)

            def spool_store(turn, half):
                g = turn * 2 + half
                sp.dma_start(spool_view[bass.ds(g, 1), :, :, :].rearrange("o p c w -> (o p) c w"),
                             Gs[:, half * CH:(half + 1) * CH, :]).then_inc(spool_stored[half], 16)

            def group_gathered(turn, half):
                for s in range(half * CH, (half + 1) * CH):
                    sp.wait_ge(gathered[s], (turn + 1) * (16 * TJ))
                sp.sem_inc(sp_passed, 1)

            idx_load(0, 0)
            idx_load(0, 1)
            if TURNS > 1:
                with sp.Fori(1, TURNS) as turn:
                    for half in range(2):
                        group_gathered(turn - 1, half)
                        idx_load(turn, half)
                        spool_store(turn - 1, half)
            for half in range(2):
                group_gathered(TURNS - 1, half)
                spool_store(TURNS - 1, half)
            for q in range(NQ):
                store_h(1, q)

            sp.wait_ge(same_stored, 32)
            sp.wait_ge(ex_stored, 32)
            sp.wait_ge(G_zeroed, 1)
            for l in range(1, 4):
                if l in MLP:
                    sp.wait_ge(h_scattered[l], 16 * B)
                ex_view = ex_row.rearrange("(g c p j) -> g p c j", c=CH, p=P, j=TJ)
                rows_view = prefix[l].rearrange("(g c p j) d -> g p c (j d)", c=CH, p=P, j=TJ)

                def load(turn, half, l=l, ex_view=ex_view):
                    g = turn * 2 + half
                    first_turn = isinstance(turn, int) and turn == 0
                    if not first_turn:
                        for s in range(half * CH, (half + 1) * CH):
                            sp.wait_ge(gathered[s], (l * TURNS + turn) * (16 * TJ))
                        sp.sem_inc(sp_passed, 1)
                    sp.dma_start(idx[:, half, :], src_in[bass.ds(g, 1), :, :].rearrange("o p k -> (o p) k"))\
                      .then_inc(idx_in[half], 16)
                    done = turn * RING + (half - 1) * CH
                    if l in MLP:
                        if not first_turn:
                            sp.wait_ge(transposed[l], done)
                            sp.sem_inc(sp_passed, 1)
                        for c in range(CH):
                            sp.dma_start(G[:, half * CH + c, :, 64:112],
                                         first_view[bass.ds(g, 1), :, c, :, :].rearrange("o p j d -> (o p) j d"))\
                              .then_inc(first_in[l][half], 16)
                        if not first_turn:
                            sp.wait_ge(hidden1[l], done)
                            sp.sem_inc(sp_passed, 1)
                        ks = K[:, half * CH:(half + 1) * CH, :].rearrange("k c n -> k (c n)")
                        sp.dma_start(ks[48:64, :], ea3_in[:, bass.ds(g * GROUP, GROUP)]).then_inc(ea_in[l][half], 16)
                    if l == 1:
                        if not first_turn:
                            sp.wait_ge(weighted[l], done)
                            sp.sem_inc(sp_passed, 1)
                        for c in range(CH):
                            sp.dma_start(ex[:, half, c, :],
                                         ex_view[bass.ds(g, 1), :, c, :].rearrange("o p j -> (o p) j"))\
                              .then_inc(ex_in[l][half], 16)
                    if not first_turn:
                        sp.wait_ge(scanned[l], done)
                        sp.sem_inc(sp_passed, 1)
                    rows = P if l in MLP else 64
                    mrow = {1: decay_row, 2: restart_row, 3: same_row}[l]
                    mdst = mask_f[0:rows, half, :] if l == 1 else mask_h[0:rows, half, 0:GROUP]
                    sp.dma_start(mdst, mrow[bass.ds(g * GROUP, GROUP)].rearrange("(o n) -> o n", o=1)
                                 .to_broadcast([rows, GROUP])).then_inc(mask_in[half], 16)

                def store(turn, half, l=l, rows_view=rows_view):
                    g = turn * 2 + half
                    sp.wait_ge(rows_copied[l], turn * RING + (half + 1) * CH)
                    sp.sem_inc(sp_passed, 1)
                    W = TJ * widths[l]
                    sp.dma_start(rows_view[bass.ds(g, 1), :, :, :].rearrange("o p c w -> (o p) c w"),
                                 O[:, half * CH:(half + 1) * CH, 0:W]).then_inc(rows_stored[half], 16)

                load(0, 0)
                load(0, 1)
                if TURNS > 1:
                    with sp.Fori(1, TURNS) as turn:
                        for half in range(2):
                            load(turn, half)
                            store(turn - 1, half)
                store(TURNS - 1, 0)
                store(TURNS - 1, 1)
                if l < 3:
                    for q in range(NQ):
                        store_h(l + 1, q)
            for q in range(NQ):
                sp.wait_ge(out_made, q + 1)
                bs = slice(q * NODE_BLOCKS, (q + 1) * NODE_BLOCKS)
                sp.dma_start(out.rearrange("(p b) d -> p b d", p=P)[:, bs, :], x[:, bs, :]).then_inc(out_stored, 16)
            sp.wait_ge(out_stored, 16 * NQ)
            for half in range(2):
                sp.wait_ge(rows_stored[half], 16 * TURNS * 4)
            for l in range(4):
                sp.wait_ge(h_stored[l], 16 * NQ)
            for l in MLP:
                sp.wait_ge(h_scattered[l], 16 * B)

        @block.gpsimd
        def _(pool):
            pool.memset(ident[:, :], 0.0).then_inc(ident_set, 1)
            pool.wait_ge(ident_set, 1)
            pool.affine_select(out=ident[:, :], in_=ident[:, :], compare_op=ALU.not_equal, fill=1.0,
                               base=0, pattern=[[-1, P]], channel_multiplier=1).then_inc(ident_done, 1)
            pool.iota(low_ids_i[:, :], pattern=[[1, LO]], base=0, channel_multiplier=0).then_inc(node_id_set, 1)
            pool.iota(node_id_i[:, :], pattern=[[1, B]], base=0, channel_multiplier=B).then_inc(node_id_set, 1)
            pool.memset(above[:, :], 1.0).then_inc(ident_set, 1)
            pool.wait_ge(ident_set, 2)
            pool.affine_select(out=above[:, :], in_=above[:, :], compare_op=ALU.is_gt, fill=0.0,
                               base=0, pattern=[[1, P]], channel_multiplier=-1).then_inc(ident_done, 1)
            pool.memset(G[:, :, :, :].rearrange("p a b c -> p (a b c)"), 0.0).then_inc(G_zeroed, 1)

            def scatter(v, q):
                pool.wait_ge(h_made[v], q + 1)
                for b in range(q * NODE_BLOCKS, (q + 1) * NODE_BLOCKS):
                    pool.indirect_dma_start(first_rows, bass.IndirectOffsetOnAxis(ap=first_edge[:, b:b + 1], axis=0),
                                            h[:, b, 0:D], None).then_inc(h_scattered[v], 16)

            pool.wait_ge(G_zeroed, 1)
            for l in range(4):
                pool.wait_ge(h_stored[l], 16 * NQ)

                def gather(c, l=l):
                    if c.at_group_start:
                        pool.wait_ge(idx_in[c.half], (l * TURNS + c.turn + 1) * 16)
                    if l == 0:
                        if not (c.fixed and c.n < RING) and c.at_group_start:
                            pool.wait_ge(spool_stored[c.half], c.turn * 16)
                    elif not (c.fixed and c.n < RING):
                        pool.wait_ge(transposed[l], c.n - (RING - 1))
                    pool.sem_inc(pool_passed, 1)
                    for j in range(TJ):
                        k = (c.slot % CH) * TJ + j
                        rows = Gs[:, c.slot, j * D:(j + 1) * D] if l == 0 else G[:, c.slot, j, 0:widths[l]]
                        pool.indirect_dma_start(rows, None, table[l],
                                                bass.IndirectOffsetOnAxis(ap=idx[:, c.half, k:k + 1], axis=0))\
                            .then_inc(gathered[c.slot], 16)

                if l > 0:
                    pipeline(pool, [(0, gather)], TURNS)
                else:
                    pipeline(pool, [(0, gather)], SPLIT)
                    pool.wait_ge(places_made, 1)
                    pool.wait_ge(rows_zeroed, 16 * (EC // 16 // ZERO_STEP))
                    for q in range(NQ):
                        scatter(0, q)
                    if SPLIT < TURNS:
                        with pool.Fori(SPLIT, TURNS) as turn:
                            for k in range(RING):
                                gather(Chunk(turn, k))
                for half in range(2):
                    pool.wait_ge(rows_stored[half], 16 * TURNS * (l + 1))
                v = l + 1
                for q in range(NQ):
                    if q >= 2:
                        pool.wait_ge(last_rows_used[v], q - 1)
                    for k in range(NODE_BLOCKS):
                        b = q * NODE_BLOCKS + k
                        pool.indirect_dma_start(R[:, q % 2, k, 0:widths[l]], None, prefix[l],
                                                bass.IndirectOffsetOnAxis(ap=last_edge[:, b:b + 1], axis=0))\
                            .then_inc(last_rows_in[v][q % 2], 16)
                    if v == 3 and q:
                        scatter(3, q - 1)
                if v == 3:
                    scatter(3, NQ - 1)

        @block.scalar
        def _(act):
            def sqrt_var(v, q):
                act.wait_ge(var_made[v], q + 1)
                act.activation(ns[:, q % 2, 2, :], ns[:, q % 2, 1, :], ACT.Sqrt, bias=eps[:, :], scale=1.0 / D)\
                   .then_inc(sd_made[v], 1)

            act.dma_start(e_w[:, :], w_in.rearrange("(p c) -> p c", p=P)).then_inc(w_edge_in, 16)
            for part, data in weight_loads:
                act.dma_start(part, data).then_inc(weights_in, 16)
            for q in range(NQ):
                sqrt_var(0, q)
            act.wait_ge(same_made, 2)
            act.dma_start(same_row.rearrange("(p c) -> p c", p=P), e_half[:, :]).then_inc(same_stored, 16)
            act.dma_start(restart_row.rearrange("(p c) -> p c", p=P), e_half2[:, :]).then_inc(same_stored, 16)
            act.wait_ge(zeros_set, 1)
            zero_view = first_rows[0:E, :].rearrange("(p r q) d -> p r (q d)", p=P, q=16)
            for n, r in enumerate(range(0, EC // 16, ZERO_STEP)):
                if n:
                    act.wait_ge(rows_zeroed, 16 * n)
                act.dma_start(zero_view[:, r:r + ZERO_STEP, :],
                              zeros[:, :].rearrange("p (o q) -> p o q", o=1).to_broadcast([P, ZERO_STEP, 16 * D]))\
                   .then_inc(rows_zeroed, 16)
            act.wait_ge(ends_made, 1)
            act.dma_start(count_dram.rearrange("a (h l) -> h a l", l=LO), counts[:, :, :]).then_inc(ends_stored, 16)
            act.wait_ge(ends_stored, 16)
            act.dma_start(count[:, :], count_dram[0, :].rearrange("(p b) -> p b", p=P)).then_inc(ends_in, 16)
            act.dma_start(end[:, :], count_dram[1, :].rearrange("(p b) -> p b", p=P)).then_inc(ends_in, 16)
            act.wait_ge(carry_made, 1)
            act.dma_start(carry_dram[0:2, :].rearrange("a p -> p a"), row_stat[:, :],
                          allow_slow_non_contiguous=True).then_inc(carry_hop[0], 16)
            act.wait_ge(carry_hop[0], 16)
            act.dma_start(carry_row[:, :, :], carry_dram[0:2, :].rearrange("(o a) p -> o a p", o=1))\
               .then_inc(carry_hop[1], 16)
            act.wait_ge(carry_made, 2)
            act.dma_start(carry_dram[2:3, :], carry_scan[0:1, 0:P]).then_inc(carry_hop[2], 16)
            act.wait_ge(carry_hop[2], 16)
            act.dma_start(carry[:, :], carry_dram[2:3, :].rearrange("o p -> p o"),
                          allow_slow_non_contiguous=True).then_inc(carry_hop[3], 16)
            act.wait_ge(ex_arg_made, 1)
            act.activation(e_tmp[:, :], e_tmp[:, :], ACT.Exp).then_inc(ex_made, 1)
            act.wait_ge(ex_made, 1)
            act.dma_start(ex_row.rearrange("(p c) -> p c", p=P), e_tmp[:, :]).then_inc(ex_stored, 16)
            act.wait_ge(ex_arg_made, 2)
            act.activation(e_max[:, :], e_w[:, :], ACT.Exp).then_inc(ex_made, 1)
            act.wait_ge(decay_made, 1)
            act.dma_start(decay_row.rearrange("(p c) -> p c", p=P), e_max[:, :]).then_inc(ex_stored, 16)
            act.wait_ge(weights_in, ALL_WEIGHTS)

            def load_rows_0(turn, pair):
                half, k = divmod(2 * pair, CH)
                g = turn * 2 + half
                if k == 0:
                    act.wait_ge(spool_stored[half], (turn + 1) * 16)
                    act.sem_inc(act_passed, 1)
                for part, view in ((0, spool_view), (1, first_flat)):
                    act.dma_start(G0[:, 2 * pair:2 * pair + 2, part * TJ * D:(part + 1) * TJ * D],
                                  view[bass.ds(g, 1), :, k:k + 2, :].rearrange("o p c w -> (o p) c w"))\
                       .then_inc(rows_in[pair], 16)

            def load_features_0(turn, half):
                g = turn * 2 + half
                if not (isinstance(turn, int) and turn == 0):
                    done = turn * RING + (half - 1) * CH
                    act.wait_ge(hidden1[0], done)
                    act.wait_ge(scanned[0], done)
                    act.sem_inc(act_passed, 1)
                ks = K[:, half * CH:(half + 1) * CH, :].rearrange("k c n -> k (c n)")
                act.dma_start(ks[48:64, :], ea0_in[0:16, bass.ds(g * GROUP, GROUP)]).then_inc(ea_in[0][half], 16)
                act.dma_start(ks[112:128, :], ea0_in[16:32, bass.ds(g * GROUP, GROUP)]).then_inc(ea_in[0][half], 16)
                act.dma_start(mask_h[:, half, 0:GROUP],
                              same_row[bass.ds(g * GROUP, GROUP)].rearrange("(o n) -> o n", o=1)
                              .to_broadcast([P, GROUP])).then_inc(mask_in[half], 16)

            def next_features_0(c):
                if c.at_group_start and not (c.fixed and c.turn + 1 >= TURNS):
                    load_features_0(c.turn + 1, c.half)

            def next_rows_0(c):
                if c.slot % 2 and not (c.fixed and c.turn + 1 >= TURNS):
                    load_rows_0(c.turn + 1, c.slot // 2)

            def store_rows_0(c):
                if c.slot % CH == CH - 1:
                    act.wait_ge(rows_copied[0], c.n + 1)
                    act.sem_inc(act_passed, 1)
                    g = c.turn * 2 + c.half
                    view = prefix[0].rearrange("(g c p j) d -> g p c (j d)", c=CH, p=P, j=TJ)
                    act.dma_start(view[bass.ds(g, 1), :, :, :].rearrange("o p c w -> (o p) c w"),
                                  O[:, c.half * CH:(c.half + 1) * CH, 0:TJ * D]).then_inc(rows_stored[c.half], 16)

            act.wait_ge(same_stored, 32)
            act.wait_ge(h_scattered[0], 16 * B)
            act.wait_ge(G_zeroed, 1)
            for half in range(2):
                load_features_0(0, half)
            for pair in range(RING // 2):
                load_rows_0(0, pair)
            for l in range(4):
                def copy_src(c, l=l):
                    act.wait_ge(transposed[l], c.n + 1)
                    if not (c.fixed and c.n < RING):
                        act.wait_ge(hidden1[l], c.n - (RING - 1))
                    first = 64 if l == 0 else 0
                    act.activation(K[first:first + D, c.slot, :], pT[c.slot % 2][0:D, :], ACT.Copy).then_inc(src_copied[l], 1)

                def relu_1(c, l=l):
                    act.wait_ge(hidden1[l], c.n + 1)
                    bank = pH1[c.slot % 2]
                    if l == 0:
                        act.activation(bank[:, :], bank[:, :], ACT.Relu, bias=b1_0[:, :]).then_inc(relu1[l], 1)
                        return
                    if not (c.fixed and c.n < 4):
                        act.wait_ge(hidden2[l], c.n - 3)
                    act.activation(H1[:, c.slot % 4, :], bank[:, :], ACT.Relu, bias=b1_3[:, :])\
                       .then_inc(relu1[l], 1)

                def relu_2(c, l=l):
                    act.wait_ge(hidden2[l], c.n + 1)
                    bank = pH2[c.slot % 2]
                    act.activation(bank[:, :], bank[:, :], ACT.Relu, bias=b2_3[:, :]).then_inc(relu2[l], 1)

                def weight_rows(c, l=l):
                    act.wait_ge(gathered[c.slot], (l * TURNS + c.turn + 1) * (16 * TJ))
                    if c.at_group_start:
                        act.wait_ge(ex_in[l][c.half], (c.turn + 1) * (16 * CH))
                    for j in range(TJ):
                        g = G[:, c.slot, j, 0:D + 1]
                        last = act.activation(g, g, ACT.Copy, scale=ex[:, c.half, c.slot % CH, j:j + 1])
                    last.then_inc(weighted[l], 1)

                def copy_rows(c, l=l):
                    act.wait_ge(rows_made[l], c.n + 1)
                    if c.at_group_start and not (c.fixed and c.n < RING):
                        act.wait_ge(rows_stored[c.half], (l * TURNS + c.turn) * 16)
                    W = TJ * widths[l]
                    act.activation(O[:, c.slot, 0:W], pO[c.slot % 2][:, 0:W], ACT.Copy).then_inc(rows_copied[l], 1)

                stages = {0: [(2, next_rows_0), (6, next_features_0), (0, copy_src), (1, relu_1), (3, copy_rows),
                              (4, store_rows_0)],
                          1: [(0, weight_rows), (3, copy_rows)],
                          2: [(0, copy_src), (3, copy_rows)],
                          3: [(0, copy_src), (1, relu_1), (3, copy_rows), (1, relu_2)]}[l]
                pipeline(act, stages, TURNS, TURNS - 1 if l == 0 else TURNS)
                v = l + 1
                for q in range(NQ):
                    if v == 2:
                        act.wait_ge(elu_arg, q + 1)
                        act.activation(u2[:, q % 2, :, :], u2[:, q % 2, :, :], ACT.Exp).then_inc(elu_exp, 1)
                    if v == 3:
                        for i in range(2):
                            act.wait_ge(hT_made, 2 * q + i + 1)
                            if q:
                                act.wait_ge(theta_h, q)
                            act.activation(K[0:D, i, :], pT[i][0:D, :], ACT.Copy).then_inc(hT_copied, 1)
                    if v < 4:
                        sqrt_var(v, q)

        @block.tensor
        def _(pe):
            def count_edges(k, start, stop):
                last = pe.matmul(pO[0][0:HI, 0:LO], high_hot[:, k, 0:HI], low_hot[:, k, :], start=start, stop=stop)
                if k % HALF == HALF - 1:
                    last.then_inc(hot_counted, 1)

            HALF = COUNT_COLS // 2
            steps = EC // COUNT_COLS
            for k in range(COUNT_COLS):
                if k % HALF == 0:
                    pe.wait_ge(hot_made, k // HALF + 1)
                count_edges(k, k == 0, False)
            if steps > 2:
                with pe.Fori(1, steps - 1) as i:
                    for k in range(COUNT_COLS):
                        if k % HALF == 0:
                            pe.wait_ge(hot_made, i * 2 + (k // HALF + 1))
                        count_edges(k, False, False)
            for k in range(COUNT_COLS):
                if k % HALF == 0:
                    pe.wait_ge(hot_made, (steps - 1) * 2 + k // HALF + 1)
                count_edges(k, False, k == COUNT_COLS - 1)
            pe.wait_ge(ident_done, 2)
            pe.wait_ge(totals_made, 1)
            pe.matmul(pO[1][0:HI, 0:1], above[0:HI, 0:HI], row_total[:, :], start=True, stop=True)\
              .then_inc(totals_summed, 1)
            pe.wait_ge(G_zeroed, 1)
            pe.wait_ge(weights_in, ALL_WEIGHTS)
            for l in range(4):
                rows_T = 112 if l in MLP else widths[l]

                def transpose_rows(c, l=l, rows_T=rows_T):
                    if l > 0:
                        pe.wait_ge(gathered[c.slot], (l * TURNS + c.turn + 1) * (16 * TJ))
                    elif c.slot % 2 == 0:
                        pe.wait_ge(rows_in[c.slot // 2], (c.turn + 1) * 32)
                    if l == 3 and c.at_group_start:
                        pe.wait_ge(first_in[l][c.half], (c.turn + 1) * (16 * CH))
                    if l == 1:
                        pe.wait_ge(weighted[l], c.n + 1)
                    if not (c.fixed and c.n < 2):
                        if l in MLP:
                            pe.wait_ge(dst_spread[l], c.n - 1)
                        if l != 1:
                            pe.wait_ge(src_copied[l], c.n - 1)
                        else:
                            pe.wait_ge(scanned[l], c.n - 1)
                    pe.sem_inc(pe_passed, 1)
                    o = pT[c.slot % 2][:, :].rearrange("k (p j) -> k p j", j=TJ)
                    oX = pH2[c.slot % 2][:, :].rearrange("k (p j) -> k p j", j=TJ)
                    for j in range(TJ):
                        if l == 0:
                            pe.transpose(o[0:D, :, j], G0[:, c.slot, j * D:(j + 1) * D], ident[:, :])
                            last = pe.transpose(oX[0:D, :, j], G0[:, c.slot, (TJ + j) * D:(TJ + j + 1) * D],
                                                ident[:, :])
                        else:
                            last = pe.transpose(o[0:rows_T, :, j], G[:, c.slot, j, 0:rows_T], ident[:, :])
                    last.then_inc(transposed[l], 1)

                def layer_1(c, l=l):
                    pe.wait_ge(src_copied[l], c.n + 1)
                    if l in MLP:
                        pe.wait_ge(dst_spread[l], c.n + 1)
                        if c.at_group_start:
                            pe.wait_ge(ea_in[l][c.half], (c.turn + 1) * (32 if l == 0 else 16))
                    if not (c.fixed and c.n < 2):
                        pe.wait_ge(relu1[l] if l == 3 else scanned[l], c.n - 1)
                    if l in MLP:
                        k = KROWS[l]
                        w = w1_0 if l == 0 else w1_3
                        pe.matmul(pH1[c.slot % 2][:, :], w[0:k, :], K[0:k, c.slot, :], start=True, stop=True)\
                          .then_inc(hidden1[l], 1)
                    else:
                        pe.sem_inc(pe_passed, 1)
                        pe.matmul(pH1[c.slot % 2][0:D, :], wq[:, :], K[0:D, c.slot, :], start=True, stop=True)\
                          .then_inc(hidden1[l], 1)

                def layer_2(c, l=l):
                    pe.wait_ge(relu1[l], c.n + 1)
                    if not (c.fixed and c.n < 2):
                        pe.wait_ge(scanned[l], c.n - 1)
                    pe.matmul(pH2[c.slot % 2][:, :], w2_3[:, :], H1[:, c.slot % 4, :], start=True, stop=True)\
                      .then_inc(hidden2[l], 1)

                def make_rows(c, l=l):
                    pe.wait_ge(scanned[l], c.n + 1)
                    if not (c.fixed and c.n < 2):
                        pe.wait_ge(rows_copied[l], c.n - 1)
                    pe.sem_inc(pe_passed, 1)
                    w = widths[l]
                    s = S[:, c.slot % 4, :].rearrange("k (p j) -> k p j", j=TJ)
                    for j in range(TJ):
                        o = pO[c.slot % 2][:, j * w:(j + 1) * w]
                        if l in MLP:
                            last = pe.matmul(o, s[:, :, j], (w2_0 if l == 0 else w3_3)[:, :], start=True, stop=True)
                        else:
                            last = pe.transpose(o, s[0:w, :, j], ident[0:w, 0:w])
                    last.then_inc(rows_made[l], 1)

                if l == 2:
                    pe.wait_ge(wq_made, 1)
                stages = {0: [(0, transpose_rows), (1, layer_1), (3, make_rows)],
                          1: [(0, transpose_rows), (3, make_rows)],
                          2: [(0, transpose_rows), (1, layer_1), (3, make_rows)],
                          3: [(0, transpose_rows), (1, layer_1), (3, make_rows), (1, layer_2)]}[l]
                pipeline(pe, stages, TURNS)
                if l == 2:
                    pe.wait_ge(src_copied[2], NCH)
                    pe.wait_ge(rows_copied[2], NCH)
                    for q in range(NQ):
                        for i in range(2):
                            if q:
                                pe.wait_ge(hT_copied, 2 * (q - 1) + i + 1)
                            ks = range(i * 4, min(NODE_BLOCKS, i * 4 + 4))
                            for k in ks:
                                last = pe.transpose(pT[i][0:D, (k - 4 * i) * P:(k - 4 * i + 1) * P],
                                                    h[:, q * NODE_BLOCKS + k, 0:D], ident[:, :])
                            last.then_inc(hT_made, 1)
                        pe.wait_ge(hT_copied, 2 * q + 2)
                        if q >= 2:
                            pe.wait_ge(last_rows_used[3], q - 1)
                        for k in range(NODE_BLOCKS):
                            last = pe.matmul(pO[q % 2][:, k * D:(k + 1) * D],
                                             K[0:D, k // 4, (k % 4) * P:(k % 4 + 1) * P], thetaT[:, :],
                                             start=True, stop=True)
                        last.then_inc(theta_h, 1)

        @block.vector
        def _(dve):
            own = [0]

            def link(ins):
                own[0] += 1
                ins.then_inc(vector_done, 1)
                dve.wait_ge(vector_done, own[0])

            dve.memset(zeros[:, :], 0.0).then_inc(zeros_set, 1)
            link(dve.memset(eps[:, :], 1e-5))
            link(dve.memset(h[:, :, D:D + 1], 1.0))
            link(dve.memset(K[:, RING - 1, CHUNK - 1:CHUNK], 0.0))
            link(dve.memset(S[:, 3, CHUNK - 1:CHUNK], 0.0))
            def over_features(v):
                return v.rearrange("p (b o) -> p b o", o=1).to_broadcast([P, NODE_BLOCKS, D])

            def layernorm(v, q):
                bs = slice(q * NODE_BLOCKS, (q + 1) * NODE_BLOCKS)
                s = q % 2
                link(dve.tensor_reduce(ns[:, s, 0, :], x[:, bs, :], AX, ALU.add))
                link(dve.tensor_scalar(ns[:, s, 0, :], ns[:, s, 0, :], 1.0 / D, None, ALU.mult))
                link(dve.tensor_tensor(u[:, s, :, :], x[:, bs, :], over_features(ns[:, s, 0, :]), ALU.subtract))
                link(dve.tensor_tensor(u2[:, s, :, :], u[:, s, :, :], u[:, s, :, :], ALU.mult))
                dve.tensor_reduce(ns[:, s, 1, :], u2[:, s, :, :], AX, ALU.add).then_inc(var_made[v], 1)

            def finish_norm(v, q):
                bs = slice(q * NODE_BLOCKS, (q + 1) * NODE_BLOCKS)
                s = q % 2
                dve.wait_ge(sd_made[v], q + 1)
                link(dve.reciprocal(ns[:, s, 3, :], ns[:, s, 2, :]))
                dve.scalar_tensor_tensor(h[:, bs, 0:D], u[:, s, :, :], 0.0, over_features(ns[:, s, 3, :]),
                                         ALU.max, ALU.mult).then_inc(h_made[v], 1)

            for q in range(NQ):
                if q < 2:
                    dve.wait_ge(x_loaded[q], 16)
                layernorm(0, q)
                if q:
                    finish_norm(0, q - 1)
            finish_norm(0, NQ - 1)

            dve.wait_ge(edges_in, 32)
            link(dve.tensor_tensor(e_start[:, :], e_dst[:, :], e_prev[:, :], ALU.not_equal))
            dve.tensor_scalar(e_half[:, :], e_start[:, :], -1.0, 1.0, ALU.mult, ALU.add).then_inc(same_made, 1)
            dve.tensor_scalar(e_half2[:, :], e_start[:, :], -BIG, None, ALU.mult).then_inc(same_made, 1)

            shift = LO.bit_length() - 1
            dve.wait_ge(node_id_set, 2)
            link(dve.tensor_copy(low_ids, low_ids_i[:, :]))
            link(dve.tensor_copy(node_id[:, :], node_id_i[:, :]))
            link(dve.tensor_scalar(e_prev[:, :], e_dst[:, :], shift, None, ALU.arith_shift_right))
            link(dve.tensor_scalar(e_dst[:, :], e_dst[:, :], LO - 1, None, ALU.bitwise_and))
            link(dve.tensor_copy(e_max[:, :], e_prev[:, :]))
            link(dve.tensor_copy(e_tmp[:, :], e_dst[:, :]))
            HALF = COUNT_COLS // 2

            def one_hots(i, fixed):
                for k in range(COUNT_COLS):
                    if k % HALF == 0 and not fixed:
                        dve.wait_ge(hot_counted, i * 2 + (k // HALF - 1))
                        dve.sem_inc(dve_passed, 1)
                    if k == 0:
                        if not fixed:
                            dve.wait_ge(hot_made, i * 2)
                        cols = bass.ds(i * COUNT_COLS, COUNT_COLS)
                        dve.tensor_copy(high_cols[:, :], e_max[:, cols]).then_inc(cols_copied, 1)
                        dve.tensor_copy(low_cols[:, :], e_tmp[:, cols]).then_inc(cols_copied, 1)
                        dve.wait_ge(cols_copied, i * 2 + 2)
                        dve.sem_inc(dve_passed, 1)
                    dve.tensor_scalar(high_hot[:, k, :], low_ids, high_cols[:, k:k + 1], None, ALU.is_equal)
                    last = dve.tensor_scalar(low_hot[:, k, :], low_ids, low_cols[:, k:k + 1], None,
                                             ALU.is_equal)
                    if k % HALF == HALF - 1:
                        last.then_inc(hot_made, 1)

            steps = EC // COUNT_COLS
            one_hots(0, True)
            with dve.Fori(1, steps) as i:
                one_hots(i, False)
            dve.wait_ge(hot_counted, 2 * steps)
            link(dve.tensor_copy(counts[:, 0, :], pO[0][0:HI, 0:LO]))
            dve.tensor_reduce(row_total[:, :], counts[:, 0, :], AX, ALU.add).then_inc(totals_made, 1)
            link(dve.memset(high_hot[:, 0, :], 1.0))
            dve.wait_ge(totals_summed, 1)
            link(dve.tensor_copy(row_total[:, :], pO[1][0:HI, 0:1]))
            dve.tensor_tensor_scan(counts[:, 1, :], high_hot[0:HI, 0, :], counts[:, 0, :], row_total[:, :],
                                   ALU.mult, ALU.add).then_inc(ends_made, 1)
            dve.wait_ge(ends_in, 32)
            link(dve.tensor_scalar(filled[:, :], count[:, :], 0.0, None, ALU.is_gt))
            link(dve.tensor_scalar(empty[:, :], filled[:, :], -1.0, 1.0, ALU.mult, ALU.add))
            link(dve.tensor_scalar(last_edge[:, :], end[:, :], -1.0, 0.0, ALU.add, ALU.max))
            link(dve.tensor_scalar(node_tmp[:, :], count[:, :], 1.0, None, ALU.max))
            link(dve.reciprocal(inv_count[:, :], node_tmp[:, :]))
            link(dve.tensor_tensor(end[:, :], end[:, :], count[:, :], ALU.subtract))
            link(dve.tensor_scalar(node_id[:, :], node_id[:, :], float(E), None, ALU.add))
            link(dve.tensor_tensor(end[:, :], end[:, :], node_id[:, :], ALU.subtract))
            link(dve.tensor_tensor(end[:, :], end[:, :], filled[:, :], ALU.mult))
            dve.tensor_tensor(first_edge[:, :], end[:, :], node_id[:, :], ALU.add).then_inc(places_made, 1)

            dve.wait_ge(w_edge_in, 16)
            link(dve.tensor_scalar(e_tmp[:, :], e_start[:, :], -BIG, None, ALU.mult))
            link(dve.tensor_tensor_scan(e_max[:, :], e_tmp[:, :], e_w[:, :], -BIG, ALU.add, ALU.max))
            link(dve.tensor_copy(row_stat[:, 1:2], e_max[:, EC - 1:EC]))
            dve.tensor_reduce(row_stat[:, 0:1], e_tmp[:, :], AX, ALU.min).then_inc(carry_made, 1)
            link(dve.memset(carry_scan[:, 0:1], -BIG))
            dve.wait_ge(carry_hop[1], 16)
            dve.tensor_tensor_scan(carry_scan[:, 1:P + 1], carry_row[:, 0, :], carry_row[:, 1, :], -BIG,
                                   ALU.add, ALU.max).then_inc(carry_made, 1)
            dve.wait_ge(carry_hop[3], 16)
            link(dve.tensor_tensor_scan(e_max[:, :], e_tmp[:, :], e_w[:, :], carry[:, :], ALU.add, ALU.max))
            dve.tensor_tensor(e_tmp[:, :], e_w[:, :], e_max[:, :], ALU.subtract).then_inc(ex_arg_made, 1)
            dve.wait_ge(ex_made, 1)
            link(dve.tensor_tensor(e_w[:, 1:EC], e_max[:, 0:EC - 1], e_max[:, 1:EC], ALU.subtract))
            link(dve.tensor_tensor(e_w[:, 0:1], carry[:, :], e_max[:, 0:1], ALU.subtract))
            dve.tensor_scalar(e_w[:, :], e_w[:, :], 0.0, None, ALU.min).then_inc(ex_arg_made, 1)
            dve.wait_ge(ex_made, 2)
            link(dve.tensor_scalar(e_start[:, :], e_start[:, :], -1.0, 1.0, ALU.mult, ALU.add))
            dve.tensor_tensor(e_max[:, :], e_max[:, :], e_start[:, :], ALU.mult).then_inc(decay_made, 1)

            dve.wait_ge(weights_in, ALL_WEIGHTS)
            dve.tensor_tensor(wq[:, :], phiT[:, :], thetaT[:, :], ALU.subtract).then_inc(wq_made, 1)
            link(dve.tensor_tensor(tb[:, :, :], tb[:, :, :], pb[:, :, :], ALU.add))

            for l in range(4):
                def mask_of(c, rows, l=l):
                    m = mask_f if l == 1 else mask_h
                    k = c.slot % CH
                    return m[rows, c.half, k * CHUNK:(k + 1) * CHUNK]

                def spread_dst(c, l=l):
                    if c.at_group_start:
                        dve.wait_ge(mask_in[c.half], (l * TURNS + c.turn + 1) * 16)
                    dve.wait_ge(transposed[l], c.n + 1)
                    if not (c.fixed and c.n == 0):
                        dve.wait_ge(dst_spread[l], c.n)
                    if not (c.fixed and c.n < RING):
                        dve.wait_ge(hidden1[l], c.n - (RING - 1))
                    r = slice(0, D) if l == 0 else slice(64, 64 + D)
                    first_T = (pH2 if l == 0 else pT)[c.slot % 2]
                    dve.tensor_tensor_scan(K[r, c.slot, :], mask_of(c, r), first_T[r, :],
                                           K[r, (c.slot - 1) % RING, CHUNK - 1:CHUNK], ALU.mult, ALU.add)\
                       .then_inc(dst_spread[l], 1)

                def scan(c, l=l):
                    if l not in MLP and c.at_group_start:
                        dve.wait_ge(mask_in[c.half], (l * TURNS + c.turn + 1) * 16)
                    dve.wait_ge({0: relu1, 1: transposed, 2: hidden1, 3: relu2}[l][l], c.n + 1)
                    if not (c.fixed and c.n == 0):
                        dve.wait_ge(scanned[l], c.n)
                    if not (c.fixed and c.n < 4):
                        dve.wait_ge(rows_made[l], c.n - 3)
                    r = slice(0, P if l in MLP else widths[l])
                    data = {0: pH1, 1: pT, 2: pH1, 3: pH2}[l][c.slot % 2][r, :]
                    op0, op1 = (ALU.add, ALU.max) if l == 2 else (ALU.mult, ALU.add)
                    dve.tensor_tensor_scan(S[r, c.slot % 4, :], mask_of(c, r), data,
                                           S[r, (c.slot - 1) % 4, CHUNK - 1:CHUNK], op0, op1)\
                       .then_inc(scanned[l], 1)

                stages = {0: [(0, spread_dst), (2, scan)],
                          1: [(1, scan)],
                          2: [(2, scan)],
                          3: [(0, spread_dst), (2, scan)]}[l]
                pipeline(dve, stages, TURNS)

                v = l + 1
                for q in range(NQ + 1):
                    if v < 4 and q:
                        finish_norm(v, q - 1)
                    if q == NQ:
                        break
                    s = q % 2
                    bs = slice(q * NODE_BLOCKS, (q + 1) * NODE_BLOCKS)
                    rows = R[:, s, :, 0:D]
                    dve.wait_ge(last_rows_in[v][s], (q // 2 + 1) * 16 * NODE_BLOCKS)
                    if v == 1:
                        link(dve.tensor_tensor(u[:, s, :, :], rows, over_features(filled[:, bs]), ALU.mult))
                        link(dve.tensor_tensor(x[:, bs, :], x[:, bs, :], u[:, s, :, :], ALU.add))
                        link(dve.tensor_tensor(u2[:, s, :, :], over_features(count[:, bs]),
                                               b2_0[:, :, :].to_broadcast([P, NODE_BLOCKS, D]), ALU.mult))
                        dve.tensor_tensor(x[:, bs, :], x[:, bs, :], u2[:, s, :, :], ALU.add)\
                           .then_inc(last_rows_used[v], 1)
                        dve.wait_ge(last_rows_used[v], q + 1)
                    elif v == 2:
                        den = ns[:, s, 4, :]
                        link(dve.tensor_tensor(den, R[:, s, :, D], filled[:, bs], ALU.mult))
                        link(dve.tensor_tensor(den, den, empty[:, bs], ALU.add))
                        link(dve.reciprocal(ns[:, s, 5, :], den))
                        link(dve.tensor_tensor(ns[:, s, 5, :], ns[:, s, 5, :], filled[:, bs], ALU.mult))
                        link(dve.tensor_tensor(u[:, s, :, :], rows, over_features(ns[:, s, 5, :]), ALU.mult))
                        dve.tensor_scalar(u2[:, s, :, :], u[:, s, :, :], 0.0, None, ALU.min).then_inc(elu_arg, 1)
                        dve.wait_ge(elu_exp, q + 1)
                        link(dve.scalar_tensor_tensor(u[:, s, :, :], u[:, s, :, :], 0.0, u2[:, s, :, :],
                                                      ALU.max, ALU.add))
                        dve.scalar_tensor_tensor(x[:, bs, :], u[:, s, :, :], -1.0, x[:, bs, :], ALU.add, ALU.add)\
                           .then_inc(last_rows_used[v], 1)
                        dve.wait_ge(last_rows_used[v], q + 1)
                    elif v == 3:
                        dve.wait_ge(theta_h, q + 1)
                        link(dve.tensor_tensor(u[:, s, :, :], rows,
                                               pO[s][:, 0:NODE_BLOCKS * D].rearrange("p (b d) -> p b d", d=D), ALU.add))
                        link(dve.tensor_tensor(u[:, s, :, :], u[:, s, :, :],
                                               tb[:, :, :].to_broadcast([P, NODE_BLOCKS, D]), ALU.add))
                        link(dve.tensor_tensor(u[:, s, :, :], u[:, s, :, :], over_features(filled[:, bs]), ALU.mult))
                        dve.tensor_tensor(x[:, bs, :], x[:, bs, :], u[:, s, :, :], ALU.add)\
                           .then_inc(last_rows_used[v], 1)
                        dve.wait_ge(last_rows_used[v], q + 1)
                    else:
                        link(dve.tensor_tensor(u[:, s, :, :], rows, over_features(inv_count[:, bs]), ALU.mult))
                        link(dve.tensor_tensor(u[:, s, :, :], u[:, s, :, :],
                                               b3_3[:, :, :].to_broadcast([P, NODE_BLOCKS, D]), ALU.add))
                        dve.tensor_tensor(u[:, s, :, :], u[:, s, :, :], over_features(filled[:, bs]), ALU.mult)\
                           .then_inc(last_rows_used[v], 1)
                        dve.wait_ge(last_rows_used[v], q + 1)
                        link(dve.tensor_tensor(u[:, s, :, :], u[:, s, :, :], h[:, bs, 0:D], ALU.add))
                        dve.tensor_tensor(x[:, bs, :], x[:, bs, :], u[:, s, :, :], ALU.add).then_inc(out_made, 1)
                    if v < 4:
                        layernorm(v, q)


def kernel(**inputs):
    import numpy as np
    import concourse.bacc as _bacc
    from concourse import mybir as _mybir
    from concourse.bass_utils import run_bass_kernel_spmd as _run

    x = np.asarray(inputs["x"])
    n_nodes = x.shape[0]
    blocks = -(-n_nodes // (P * NODE_BLOCKS)) * NODE_BLOCKS
    N = P * blocks
    assert N > n_nodes
    edges = np.asarray(inputs["src"]).shape[0]
    E = -(-edges // (2 * GROUP)) * 2 * GROUP

    def padded(a, fill):
        a = np.asarray(a)
        return np.concatenate([a, np.full((E - edges,) + a.shape[1:], fill, a.dtype)])

    src = padded(inputs["src"], 0)
    dst = padded(inputs["dst"], n_nodes)
    arrays = {
        "x": np.concatenate([x, np.zeros((N - n_nodes, D), x.dtype)]),
        "src": np.ascontiguousarray(src.reshape(-1, CH, P, TJ).transpose(0, 2, 1, 3)).reshape(-1, P, CH * TJ),
        "dst": dst,
        "dst_prev": np.concatenate([np.full((1,), -1, dst.dtype), dst[:-1]]),
        "ea0": np.ascontiguousarray(padded(inputs["edge_attr_32"], 0).T),
        "ea3": np.ascontiguousarray(padded(inputs["edge_attr_16"], 0).T),
        "w": padded(inputs["edge_weight1"], 0)[:, 0],
        "L0_W1": inputs["L0_gnn_W1"], "L0_b1": inputs["L0_gnn_b1"],
        "L0_W2": inputs["L0_gnn_W2"], "L0_b2": inputs["L0_gnn_b2"],
        "thetaT": np.asarray(inputs["L2_gnn_theta_w"]).T, "phiT": np.asarray(inputs["L2_gnn_phi_w"]).T,
        "theta_b": inputs["L2_gnn_theta_b"], "phi_b": inputs["L2_gnn_phi_b"],
        "L3_W1": inputs["L3_gnn_W1"], "L3_b1": inputs["L3_gnn_b1"],
        "L3_W2": inputs["L3_gnn_W2"], "L3_b2": inputs["L3_gnn_b2"],
        "L3_W3": inputs["L3_gnn_W3"], "L3_b3": inputs["L3_gnn_b3"],
    }
    nc = _bacc.Bacc("TRN2", target_bir_lowering=False, num_devices=1)
    given, args = {}, []
    for name, a in arrays.items():
        a = np.ascontiguousarray(a)
        given[f"in_{name}_dram"] = a
        args.append(nc.dram_tensor(f"in_{name}_dram", a.shape, _mybir.dt.from_np(a.dtype), kind="ExternalInput").ap())
    args.append(nc.dram_tensor("out_dram", (N, D), _mybir.dt.float32, kind="ExternalOutput").ap())
    build(nc, *args)
    r = _run(nc, [given], core_ids=[0])
    return r.results[0]["out_dram"][:n_nodes]
```
